# Optimizing a Trainium2 kernel written in Bass

```python
import numpy as np
import jax
import jax.numpy as jnp

def _softmax(x, axis=-1):
    return jax.nn.softmax(x, axis=axis)

def _gelu(x):
    return jax.nn.gelu(x, approximate=True)

def _silu(x):
    return jax.nn.silu(x)

def _sigmoid(x):
    return jax.nn.sigmoid(x)

def _layernorm(x, axis=-1, eps=1e-05):
    m = jnp.mean(x, axis=axis, keepdims=True)
    v = jnp.var(x, axis=axis, keepdims=True)
    return (x - m) / jnp.sqrt(v + eps)

def _scatter_add(tgt, idx, src, axis=0):
    return tgt.at[idx].add(src)

def _segment_sum(src, seg, n):
    return jax.ops.segment_sum(src, seg, n)
kernel_name = 'mk_xattn_ffn_d1_seqx_r8_3afa29'

def setup_inputs(seed: int=0):
    np.random.seed(seed)
    _w = jnp.asarray

    def _rec_inputs():
        import jax
        import jax.numpy as jnp
        _rk = jax.random.key(seed)
        x = -0.000125 + 0.9999 * jax.random.normal(jax.random.fold_in(_rk, 1), (4, 256, 256), jnp.float32)
        _lenS = 256 - jax.random.randint(jax.random.fold_in(_rk, 7), (4,), 0, max(1, 256 // 4) + 1, jnp.int32)
        _lenS2 = 256 - jax.random.randint(jax.random.fold_in(_rk, 8), (4,), 0, max(1, 256 // 4) + 1, jnp.int32)
        itok_BxS_13_99985 = jax.random.randint(jax.random.fold_in(_rk, 11), (4, 256), 13, 99986, jnp.int32)
        _ctx_2048P = jax.random.normal(jax.random.fold_in(_rk, 12), (4, 16, 256), jnp.float32)
        _ctx_2048c = jax.random.dirichlet(jax.random.fold_in(_rk, 512), 0.3 * jnp.ones((16,), jnp.float32), (4, 256))
        _ctx_2048t = jnp.einsum('bsk,bkd->bsd', _ctx_2048c, _ctx_2048P)
        _ctx_2048t = _ctx_2048t * jax.lax.rsqrt(jnp.mean(jnp.square(_ctx_2048t)) + 1e-12) * 0.953939
        ctx_2048 = 6.82029e-06 + 0.0200006 * (_ctx_2048t + 0.3 * jax.random.normal(jax.random.fold_in(_rk, 612), (4, 256, 256), jnp.float32))
        return (x, itok_BxS_13_99985, ctx_2048)
    x, itok_BxS_13_99985, ctx_2048 = _rec_inputs()

    def _L0_xattn_setup():
        import jax, jax.numpy as jnp
        import numpy as np
        B, S, D = (4, 512, 256)
        E = 4
        F = 1024 // E
        VOCAB = 12500
        key = jax.random.key(seed)
        k1, k2, k3, k4, k5 = jax.random.split(key, 5)
        hidden_states = jax.random.normal(k1, (B, S, D), dtype=jnp.float32)
        token_ids = jax.random.randint(k2, (B, S), 0, VOCAB, dtype=jnp.int64)
        Wg = jax.random.normal(k3, (E, F, D), dtype=jnp.float32) * 0.02
        Wu = jax.random.normal(k4, (E, F, D), dtype=jnp.float32) * 0.02
        Wd = jax.random.normal(k5, (E, D, F), dtype=jnp.float32) * 0.02
        return {'hidden_states': hidden_states, 'token_ids': token_ids, 'Wg': Wg, 'Wu': Wu, 'Wd': Wd}
    _L0_xattn_all = _L0_xattn_setup()
    _L0_xattn_in = {k: v for k, v in _L0_xattn_all.items() if k in ()}
    del _L0_xattn_all

    def _L0_ffn_setup():
        import jax, jax.numpy as jnp
        import numpy as np
        B, S, DIM = (2, 256, 256)
        E, K = (8, 2)
        H = DIM * 4 // 3
        key = jax.random.key(seed)
        ks = jax.random.split(key, 8)
        s = 0.02
        x = jax.random.normal(ks[0], (B, S, DIM), dtype=jnp.float32)
        sw1 = jax.random.normal(ks[1], (H, DIM), dtype=jnp.float32) * s
        sw2 = jax.random.normal(ks[2], (DIM, H), dtype=jnp.float32) * s
        sw3 = jax.random.normal(ks[3], (H, DIM), dtype=jnp.float32) * s
        ew1 = jax.random.normal(ks[4], (E, H, DIM), dtype=jnp.float32) * s
        ew2 = jax.random.normal(ks[5], (E, DIM, H), dtype=jnp.float32) * s
        ew3 = jax.random.normal(ks[6], (E, H, DIM), dtype=jnp.float32) * s
        wr = jax.random.normal(ks[7], (E, DIM), dtype=jnp.float32) * s
        return {'x': x, 'sw1': sw1, 'sw2': sw2, 'sw3': sw3, 'ew1': ew1, 'ew2': ew2, 'ew3': ew3, 'wr': wr}
    _L0_ffn_all = _L0_ffn_setup()
    _L0_ffn_in = {k: v for k, v in _L0_ffn_all.items() if k in ('sw1', 'sw2', 'sw3', 'ew1', 'ew2', 'ew3', 'wr')}
    del _L0_ffn_all
    return {'x': x, 'itok_BxS_13_99985': itok_BxS_13_99985, 'ctx_2048': ctx_2048, 'L0_ffn_sw1': _L0_ffn_in['sw1'], 'L0_ffn_sw2': _L0_ffn_in['sw2'], 'L0_ffn_sw3': _L0_ffn_in['sw3'], 'L0_ffn_ew1': _L0_ffn_in['ew1'], 'L0_ffn_ew2': _L0_ffn_in['ew2'], 'L0_ffn_ew3': _L0_ffn_in['ew3'], 'L0_ffn_wr': _L0_ffn_in['wr']}

def reference(x, itok_BxS_13_99985, ctx_2048, L0_ffn_sw1, L0_ffn_sw2, L0_ffn_sw3, L0_ffn_ew1, L0_ffn_ew2, L0_ffn_ew3, L0_ffn_wr):
    import jax
    import jax.numpy as jnp

    def _L0_xattn_ref(hidden_states, token_ids, Wg, Wu, Wd):
        import jax, jax.numpy as jnp
        import numpy as np
        B, S, D = (4, 512, 256)
        E = 4
        F = 1024 // E
        VOCAB = 12500
        tokens_per_expert = VOCAB // E
        tid = jnp.clip(token_ids, 0, VOCAB - 1)
        expert_ids = jnp.minimum(tid // tokens_per_expert, E - 1)
        out = jnp.zeros_like(hidden_states)
        for e in range(E):
            g = jax.nn.silu(jnp.einsum('bsd,fd->bsf', hidden_states, Wg[e]))
            u = jnp.einsum('bsd,fd->bsf', hidden_states, Wu[e])
            y = jnp.einsum('bsf,df->bsd', g * u, Wd[e])
            out = jnp.where((expert_ids == e)[..., None], y, out)
        return out

    def _L0_ffn_ref(x, sw1, sw2, sw3, ew1, ew2, ew3, wr):
        import jax, jax.numpy as jnp
        import numpy as np
        B, S, DIM = (2, 256, 256)
        E, K = (8, 2)
        H = DIM * 4 // 3
        shared = jax.nn.silu(x @ sw1.T) * (x @ sw3.T) @ sw2.T
        logits = x @ wr.T
        probs = jax.nn.softmax(logits, axis=-1)
        top_p, top_i = jax.lax.top_k(probs, K)
        top_p = top_p / jnp.sum(top_p, axis=-1, keepdims=True)
        gates = jnp.sum(jax.nn.one_hot(top_i, E, dtype=x.dtype) * top_p[..., None], axis=-2)
        u = jnp.einsum('bsd,ehd->bseh', x, ew1)
        v = jnp.einsum('bsd,ehd->bseh', x, ew3)
        h = jax.nn.silu(u) * v
        eo = jnp.einsum('bseh,edh->bsed', h, ew2)
        return shared + jnp.einsum('bsed,bse->bsd', eo, gates)
    x = x + _L0_xattn_ref(_layernorm(x, axis=-1), itok_BxS_13_99985, ctx_2048, ctx_2048, ctx_2048)
    x = x + _L0_ffn_ref(_layernorm(x, axis=-1), L0_ffn_sw1, L0_ffn_sw2, L0_ffn_sw3, L0_ffn_ew1, L0_ffn_ew2, L0_ffn_ew3, L0_ffn_wr)
    return x

_drawn_inputs = setup_inputs


def setup_inputs(seed=0):
    import zlib

    import numpy as np

    out = dict(_drawn_inputs(seed))
    spreads = {}
    factors = {'L0_ffn_ew1': 4.108,
     'L0_ffn_ew2': 4.084,
     'L0_ffn_ew3': 4.066,
     'L0_ffn_wr': 4.71,
     'L0_ffn_sw1': 3.857,
     'L0_ffn_sw2': 3.371,
     'L0_ffn_sw3': 3.369}
    for name, (base, spread) in spreads.items():
        noise = np.random.default_rng([zlib.crc32(name.encode()), seed]).standard_normal(out[name].shape)
        drawn = base * np.exp(spread * noise) if base else spread * noise
        out[name] = jnp.asarray(drawn.astype(out[name].dtype))
    for name, factor in factors.items():
        out[name] = (out[name] * factor).astype(out[name].dtype)
    return out
```

```python
from collections import namedtuple
from contextlib import ExitStack

import concourse.bass as bass
from concourse import mybir

P = 128
T = 1024
D = 256
KD = D // P
TT = T // P
CE = 4
VOCAB = 12500
VSTEP = VOCAB // CE
E = 8
TOPK = 2
H = D * 4 // 3
HP = H + H % 2
NHC = -(-H // P)
HC = [min(c * P, H - P) for c in range(NHC)]
LAST = H - (NHC - 1) * P
RT = (TOPK * T + E * (P - 1)) // P
NT = TT + RT
EPS = 1e-5
U1 = 2 * HP
UNITS = KD + 1
UNIT_AT = [u * U1 for u in range(UNITS)] + [KD * U1 + NHC * D]
BIG = 3.0e38

fp32 = mybir.dt.float32
f32r = mybir.dt.float32r
bf16 = mybir.dt.bfloat16
i32 = mybir.dt.int32
u32 = mybir.dt.uint32
ALU = mybir.AluOpType
ACT = mybir.ActivationFunctionType
AX = mybir.AxisListType.X

Tile = namedtuple("Tile", "n p before")


def tile(g, c):
    return Tile(g * 2 + c, c % 2, g + c // 2)


def build(nc, x_d, ids_d, ctx_d, w13_d, w2_d, wr_d, out_d):
    es = ExitStack()
    with es:
        def sb(name, shape, dt=fp32):
            return es.enter_context(nc.sbuf_tensor(name, shape, dt))

        def sem(name):
            return es.enter_context(nc.semaphore(name))

        x2_dram = nc.dram_tensor("x2_rows", (T, D), fp32).ap()
        h2_dram = nc.dram_tensor("h2_rows", (T, D), fp32).ap()
        acc_dram = nc.dram_tensor("acc_rows", (T + P, D), fp32).ap()

        ctx_hi = sb("ctx_hi", [P, KD, CE * D], f32r)
        ctx_lo = sb("ctx_lo", [P, KD, CE * D], f32r)
        w13_hi = sb("w13_hi", [P, E + 1, KD * U1], f32r)
        w13_lo = sb("w13_lo", [P, E + 1, KD * U1], f32r)
        w2_hi = sb("w2_hi", [P, E + 1, NHC * D], f32r)
        w2_lo = sb("w2_lo", [P, E + 1, NHC * D], f32r)
        stage = sb("stage", [P, UNIT_AT[-1]])
        wr_sb = sb("wr_sb", [P, KD, E])

        rows = sb("rows", [P, 2, D])
        normed = sb("normed", [P, 2, D])
        inT_hi = sb("inT_hi", [P, 2, D], f32r)
        inT_lo = sb("inT_lo", [P, 2, D], f32r)
        picked = sb("picked", [P, D])
        silu = sb("silu", [P, HP])
        hid = sb("hid", [P, 2, HP])
        hidT_hi = sb("hidT_hi", [P, 2, NHC * P], f32r)
        hidT_lo = sb("hidT_lo", [P, 2, NHC * P], f32r)
        x2 = sb("x2", [P, 2, D])
        h2 = sb("h2", [P, 2, D])
        h2T = sb("h2T", [P, D])
        y_sb = normed
        stats = sb("stats", [P, 2, 6])
        mv = sb("mv", [P, 2, 2])
        rstd = sb("rstd", [P, 2])
        stats2 = sb("stats2", [P, 2, 6])
        mv2 = sb("mv2", [P, 2, 2])
        rstd2 = sb("rstd2", [P, 2])
        minus_half = sb("minus_half", [P, 1])
        var = sb("var", [P, 2])
        var2 = sb("var2", [P, 2])
        N_CONST = 12

        ids = sb("ids", [P, TT], i32)
        idf = sb("idf", [P, TT])
        ge = sb("ge", [P, CE + 1, TT])
        mine = sb("mine", [P, TT, CE])
        iota = sb("iota", [P, P])
        part = sb("part", [P, 1])
        trash = sb("trash", [P, 1])
        ntrash = sb("ntrash", [P, 1])
        tok1 = sb("tok1", [P, TT])
        k128 = sb("k128", [P, E, TT])
        jtile = sb("jtile", [P, RT, E])
        rev = sb("rev", [P, E])
        ident = sb("ident", [P, P])
        below = sb("below", [P, P], bf16)
        ones = sb("ones", [P, P], bf16)
        ones8 = sb("ones8", [P, E])
        lg = sb("lg", [P, TT, E])
        lgx = sb("lgx", [P, TT, E])
        m = sb("m", [P, TOPK, TT])
        eq = sb("eq", [P, TT, E])
        wq = sb("wq", [P, TT, E])
        best = sb("best", [P, TT])
        oh = sb("oh", [P, TOPK, TT, E])
        taken = sb("taken", [P, TT + 1, E], bf16)
        sm = sb("sm", [P, TT, E])
        ssum = sb("ssum", [P, TT])
        tp = sb("tp", [P, TOPK, TT])
        gate = sb("gate", [P, TOPK, TT])
        tpx = sb("tpx", [P, TOPK, TT, E])
        cmpk = sb("cmpk", [P, E, TT])
        ntl = sb("ntl", [P, E])
        fend = sb("fend", [P, E])
        base = sb("base", [P, E])
        slot_e = sb("slot_e", [P, TT, E])
        slot_k = sb("slot_k", [P, TOPK, TT, E])
        pos = sb("pos", [P, TOPK, TT])
        posi = sb("posi", [P, TOPK * TT], i32)
        loi = sb("loi", [P, TOPK * TT], i32)
        hii = sb("hii", [P, TOPK * TT], i32)
        lof = sb("lof", [P, TOPK * TT])
        hif = sb("hif", [P, TOPK * TT])
        cmpj = sb("cmpj", [P, RT, E])
        tef = sb("tef", [P, RT])
        te = sb("te", [P, RT], i32)
        nv = TOPK * TT * 2 * RT
        vals = stage[:, 0:nv].rearrange("p (c v r) -> p c v r", c=TOPK * TT, v=2)
        looh = stage[:, nv:nv + 4 * P].rearrange("p (b n) -> p b n", b=4)
        used = sb("used", [P, RT])
        off = sb("off", [P, RT])
        src = sb("src", [P, RT], u32)
        dst = sb("dst", [P, RT], u32)
        sgate = sb("sgate", [P, RT])

        ps = es.enter_context(nc.psum_tensor("ps", [P, 8, 512], fp32))
        ps_in = ps[:, 0, :]
        ps_up = [ps[:, 1:3, :], ps[:, 3:5, :]]
        ps_y4 = ps[:, 3:5, :]
        ps_hid = ps[:, 5, :]
        ps_y = ps[:, 6, :]
        ps_r = ps[:, 7, :]

        s_ctx = [sem(f"ctx_loaded{k}") for k in range(KD)]
        s_wr, s_ids = sem("wr_loaded"), sem("ids_loaded")
        s_ctxhi, s_ctxlo = sem("ctx_hi_done"), sem("ctx_lo_done")
        s_const, s_eye, s_pad = sem("constants"), sem("matrices_made"), sem("pads_zeroed")
        s_unit = [sem(f"unit_loaded{u}") for u in range(UNITS)]
        s_uhi, s_ulo = sem("unit_hi_done"), sem("unit_lo_done")
        s_idf, s_ge, s_mine = sem("idf"), sem("ge"), sem("mine")
        s_x = [sem("x_loaded0"), sem("x_loaded1")]
        s_xres = [sem("x_residual_loaded0"), sem("x_residual_loaded1")]
        s_var1, s_var2 = sem("var1"), sem("var2")
        s_pick0, s_pickp, s_x2p = sem("picked0"), sem("picked_part"), sem("x2_part")
        s_st1, s_mv1, s_rs1, s_n1 = sem("stats1"), sem("mv1"), sem("rstd1"), sem("normed1")
        s_A1, s_hi1, s_lo1 = sem("in_transposed1"), sem("inT_hi1"), sem("inT_lo1")
        s_B1, s_pick, s_silu1, s_hid1 = sem("up1"), sem("picked"), sem("silu1"), sem("hid1")
        s_C1, s_hhi1, s_hlo1 = sem("hid_transposed1"), sem("hidT_hi1"), sem("hidT_lo1")
        s_D1, s_acc1, s_x2 = sem("down1"), sem("x2_partial"), sem("x2_ready")
        s_st2, s_mv2, s_rs2, s_h2 = sem("stats2"), sem("mv2"), sem("rstd2"), sem("h2_ready")
        s_E1, s_h2T, s_F1, s_lg = sem("h2_transposed"), sem("h2T_copied"), sem("logits"), sem("logits_copied")
        s_stored = [sem("tile_stored0"), sem("tile_stored1")]

        s_rows = [sem("rows_loaded0"), sem("rows_loaded1")]
        s_res = [sem("residual_loaded0"), sem("residual_loaded1")]
        s_gath = [sem("rows_gathered0"), sem("rows_gathered1")]
        s_A, s_hi, s_lo = sem("in_transposed"), sem("inT_hi_done"), sem("inT_lo_done")
        s_B, s_silu, s_hid = sem("up_done"), sem("silu_done"), sem("hid_done")
        s_C, s_hhi, s_hlo = sem("hid_transposed"), sem("hidT_hi_done"), sem("hidT_lo_done")
        s_D, s_y = sem("down_done"), sem("y_ready")
        s_init = [sem("acc_written0"), sem("acc_written1")]
        s_added = sem("acc_added")

        s_dv = sem("vector_routing_step")
        s_taken, s_rank, s_te = sem("taken"), sem("ranked"), sem("tile_experts")
        s_sm, s_exp = sem("softmax_shifted"), sem("softmax_exp")
        s_vals, s_looh, s_inv = sem("vals"), sem("lo_onehot"), sem("lo_onehot_used")
        s_slots, s_fin = sem("slots_ready"), sem("out_written")
        block = es.enter_context(nc.Block())


        def unit(u, part_, e):
            return part_[0][:, e, u * U1:(u + 1) * U1] if u < KD else part_[1][:, e, :]

        def pipeline(eng, first, lo, hi, end, count, step):
            def peeled(i):
                def at(k):
                    n = i + k
                    return Tile(n, n % 2, n // 2) if 0 <= n < count else None
                step(at)
            for i in range(first, lo):
                peeled(i)
            if hi > lo:
                with eng.Fori(lo // 2, hi // 2) as g:
                    for c in (0, 1):
                        step(lambda k: tile(g, c + k))
            for i in range(hi, end):
                peeled(i)

        HI, LO = (w13_hi, w2_hi), (w13_lo, w2_lo)

        @block.sync
        def _(sp):
            def load_expert(e):
                for u in range(UNITS):
                    if e > 0:
                        sp.wait_ge(s_ulo, (e - 1) * UNITS + u + 1)
                    if u < KD:
                        to = stage[:, UNIT_AT[u]:UNIT_AT[u + 1]].rearrange("p (a h) -> p a h", a=2)
                        sp.dma_start(to[:, :, 0:H], w13_d[e, u * P:(u + 1) * P, :, :]).then_inc(s_unit[u], 16)
                    else:
                        to = stage[:, UNIT_AT[u]:UNIT_AT[u + 1]].rearrange("p (c d) -> p c d", c=NHC)
                        full = w2_d[e, 0:(NHC - 1) * P, :].rearrange("(c p) d -> p c d", p=P)
                        sp.dma_start(to[:, 0:NHC - 1, :], full).then_inc(s_unit[u], 16)
                        sp.dma_start(to[P - LAST:P, NHC - 1, :], w2_d[e, (NHC - 1) * P:H, :]).then_inc(s_unit[u], 16)

            raw = stage[:, 0:KD * CE * D].rearrange("p (k n) -> p k n", k=KD)
            for k in range(KD):
                sp.dma_start(raw[:, k, :], ctx_d[k * P:(k + 1) * P, :]).then_inc(s_ctx[k], 16)
            sp.dma_start(wr_sb[:, :, :], wr_d.rearrange("(k p) e -> p k e", p=P)).then_inc(s_wr, 16)
            for n in (0, 1):
                sp.dma_start(x2[:, n, :], x_d[bass.ts(n, P), :]).then_inc(s_xres[n], 16)
            sp.wait_ge(s_pad, 1)
            load_expert(0)
            load_expert(1)
            for t in range(TT):
                if t + 2 <= E:
                    load_expert(t + 2)
                sp.wait_ge(s_h2, t + 1)
                sp.dma_start(h2_dram[bass.ts(t, P), :], h2[:, t % 2, :]).then_inc(s_stored[t % 2], 16)
                sp.dma_start(x2_dram[bass.ts(t, P), :], x2[:, t % 2, :]).then_inc(s_stored[t % 2], 16)
                if 1 <= t < TT - 1:
                    sp.wait_ge(s_stored[(t + 1) % 2], 32 * ((t + 1) // 2))
                    sp.dma_start(x2[:, (t + 1) % 2, :], x_d[bass.ts(t + 1, P), :]).then_inc(s_xres[(t + 1) % 2], 16)

            def load_rows(j):
                sp.dma_start(rows[:, j.p, :], h2_dram[bass.ts(j.n, P), :]).then_inc(s_rows[j.p], 16)

            def load_residual(j):
                sp.dma_start(x2[:, j.p, :], x2_dram[bass.ts(j.n, P), :]).then_inc(s_res[j.p], 16)

            def shared(at):
                if at(2):
                    sp.wait_ge(s_A, at(0).n + 1)
                    load_rows(at(2))
                if j := at(-2):
                    sp.wait_ge(s_y, j.n + 1)
                    sp.dma_start(acc_dram[bass.ts(j.n, P), :], y_sb[:, j.p, :]).then_inc(s_init[j.p], 16)
                    if at(0):
                        load_residual(at(0))

            for p in (0, 1):
                sp.wait_ge(s_stored[p], 32 * (TT // 2))
            for p in (0, 1):
                load_rows(Tile(p, p, 0))
            for p in (0, 1):
                load_residual(Tile(p, p, 0))
            pipeline(sp, 0, 2, TT - 2, TT + 2, TT, shared)
            sp.wait_ge(s_added, 16 * RT)
            sp.dma_start(out_d, acc_dram[0:T, :]).then_inc(s_fin, 16)
            sp.wait_ge(s_fin, 16)

        @block.gpsimd
        def _(pool):
            pool.memset(minus_half[:, :], -0.5).then_inc(s_const, 1)
            pool.memset(ones8[:, :], 1.0).then_inc(s_const, 1)
            pool.memset(ones[:, :], 1.0).then_inc(s_const, 1)
            pool.memset(taken[:, TT, :], 0.0).then_inc(s_const, 1)
            one = dict(allow_small_or_imprecise_dtypes=True)
            pool.iota(iota[:, :], [[1, P]], base=0, channel_multiplier=0, **one).then_inc(s_const, 1)
            pool.iota(part[:, :], [[1, 1]], base=0, channel_multiplier=1, **one).then_inc(s_const, 1)
            pool.iota(trash[:, :], [[1, 1]], base=T, channel_multiplier=1, **one).then_inc(s_const, 1)
            pool.iota(ntrash[:, :], [[1, 1]], base=-(T + 1), channel_multiplier=-1, **one).then_inc(s_const, 1)
            pool.iota(tok1[:, :], [[P, TT]], base=1, channel_multiplier=1, **one).then_inc(s_const, 1)
            pool.iota(k128[:, :, :], [[0, E], [P, TT]], base=0, channel_multiplier=0, **one).then_inc(s_const, 1)
            pool.iota(jtile[:, :, :], [[1, RT], [0, E]], base=0, channel_multiplier=0, **one).then_inc(s_const, 1)
            pool.iota(rev[:, :], [[-1, E]], base=E, channel_multiplier=0, **one).then_inc(s_const, 1)

            def inverse_root(to, of, ready, done):
                pool.wait_ge(*ready)
                pool.tensor_tensor(to, of, minus_half[:, :], ALU.pow).then_inc(done, 1)

            def low(n):
                e, u = divmod(n, UNITS)
                pool.wait_ge(s_uhi, n + 1)
                pool.tensor_tensor(unit(u, LO, e), stage[:, UNIT_AT[u]:UNIT_AT[u + 1]],
                                   unit(u, HI, e).bitcast(fp32), ALU.subtract).then_inc(s_ulo, 1)

            pool.wait_ge(s_const, N_CONST)
            inverse_root(rstd[:, 0:1], var[:, 0:1], (s_var1, 1), s_rs1)
            pool.wait_ge(s_ctxlo, KD)
            pool.memset(stage[:, :], 0.0).then_inc(s_pad, 1)
            for i in range(-1, TT + 2):
                if 0 <= i - 2 < TT:
                    inverse_root(rstd2[:, i % 2:i % 2 + 1], var2[:, i % 2:i % 2 + 1], (s_var2, i - 1), s_rs2)
                if 0 <= i + 2 < TT:
                    inverse_root(rstd[:, i % 2:i % 2 + 1], var[:, i % 2:i % 2 + 1], (s_var1, i + 3), s_rs1)
                if 0 <= i <= E:
                    for u in range(UNITS):
                        low(i * UNITS + u)

            pool.wait_ge(s_slots, 2)
            for r in range(-2, RT + 2):
                if r + 2 < RT:
                    n = r + 2
                    pool.wait_ge(s_A, n + TT - 1)
                    pool.indirect_dma_start(out=rows[:, n % 2, :], out_offset=None, in_=h2_dram,
                                            in_offset=bass.IndirectOffsetOnAxis(ap=src[:, n:n + 1], axis=0),
                                            ).then_inc(s_gath[n % 2], 16)
                if r - 2 >= 0:
                    n = r - 2
                    pool.wait_ge(s_y, n + TT + 1)
                    if n == 0:
                        for p in (0, 1):
                            pool.wait_ge(s_init[p], 16 * (TT // 2))
                    else:
                        pool.wait_ge(s_added, n * 16)
                    pool.indirect_dma_start(out=acc_dram, in_=y_sb[:, n % 2, :], in_offset=None,
                                            out_offset=bass.IndirectOffsetOnAxis(ap=dst[:, n:n + 1], axis=0),
                                            compute_op=ALU.add).then_inc(s_added, 16)

        @block.scalar
        def _(act):
            def load_x(t):
                act.dma_start(rows[:, t % 2, :], x_d[bass.ts(t, P), :]).then_inc(s_x[t % 2], 16)

            def high(n):
                e, u = divmod(n, UNITS)
                act.wait_ge(s_unit[u], (16 if u < KD else 32) * (e + 1))
                act.activation(unit(u, HI, e), stage[:, UNIT_AT[u]:UNIT_AT[u + 1]], ACT.Copy).then_inc(s_uhi, 1)

            load_x(0)
            act.dma_start(ids[:, :], ids_d).then_inc(s_ids, 16)
            load_x(1)
            raw = stage[:, 0:KD * CE * D].rearrange("p (k n) -> p k n", k=KD)
            for k in range(KD):
                act.wait_ge(s_ctx[k], 16)
                act.activation(ctx_hi[:, k, :], raw[:, k, :], ACT.Copy).then_inc(s_ctxhi, 1)
            for i in range(-1, TT + 3):
                a, b, c, e = i + 1, i, i - 1, i - 2
                if 0 <= c < TT:
                    act.wait_ge(s_C1, c + 1)
                    act.activation(hidT_hi[:, c % 2, 0:D], ps_hid[:, 0:D], ACT.Copy).then_inc(s_hhi1, 1)
                if 0 <= i <= E:
                    high(i * UNITS)
                    high(i * UNITS + 1)
                if 0 <= b < TT:
                    act.wait_ge(s_B1, b + 1)
                    if b:
                        act.wait_ge(s_hid1, b)
                    act.activation(picked[:, :], ps_up[0][:, 0, 0:D], ACT.Copy,
                                   scale=mine[:, b, 0:1]).then_inc(s_pick0, 1)
                if 0 <= a < TT:
                    act.wait_ge(s_A1, a + 1)
                    act.activation(inT_hi[:, a % 2, :], ps_in[:, 0:D], ACT.Copy).then_inc(s_hi1, 1)
                    if a + 2 < TT:
                        load_x(a + 2)
                if 0 <= b < TT:
                    act.wait_ge(s_pick, b + 1)
                    act.activation(silu[:, 0:D], picked[:, :], ACT.Silu).then_inc(s_silu1, 1)
                if 0 <= i <= E:
                    high(i * UNITS + 2)
                if 0 <= e < TT:
                    act.wait_ge(s_E1, e + 1)
                    if e:
                        act.wait_ge(s_F1, e)
                    act.activation(h2T[:, :], ps_y[:, 0:D], ACT.Copy).then_inc(s_h2T, 1)
            act.wait_ge(s_sm, 1)
            act.activation(sm[:, :, :], sm[:, :, :], ACT.Exp).then_inc(s_exp, 1)

            def ffn(at):
                if j := at(-1):
                    act.wait_ge(s_C, j.n + 1)
                    act.activation(hidT_hi[:, j.p, :], ps_hid[:, 0:NHC * P], ACT.Copy).then_inc(s_hhi, 1)
                if j := at(1):
                    act.wait_ge(s_A, j.n + 1)
                    act.activation(inT_hi[:, j.p, :], ps_in[:, 0:D], ACT.Copy).then_inc(s_hi, 1)
                if j := at(0):
                    act.wait_ge(s_B, j.n + 1)
                    if not (isinstance(j.n, int) and j.n == 0):
                        act.wait_ge(s_hid, j.n)
                    act.activation(silu[:, :], ps_up[j.p][:, 0, 0:HP], ACT.Silu).then_inc(s_silu, 1)
            pipeline(act, -1, 2, NT - 1, NT + 1, NT, ffn)

        @block.vector
        def _(dve):
            steps = [0]

            def link(ins):
                steps[0] += 1
                ins.then_inc(s_dv, 1)
                dve.wait_ge(s_dv, steps[0])

            def norm_stats(rows_, n, st, mv_, var_, sst, smv, svar):
                p = n % 2
                dve.bn_stats(st[:, p, :], rows_).then_inc(sst, 1)
                dve.wait_ge(sst, n + 1)
                dve.bn_aggr(mv_[:, p, :], st[:, p, :]).then_inc(smv, 1)
                dve.wait_ge(smv, n + 1)
                dve.tensor_scalar(var_[:, p:p + 1], mv_[:, p, 1:2], EPS, None, ALU.add).then_inc(svar, 1)

            def norm(out, rows_, n, mv_, rs, srs, done):
                p = n % 2
                dve.wait_ge(srs, n + 1)
                dve.tensor_scalar(out, rows_, mv_[:, p, 0:1], rs[:, p:p + 1], ALU.subtract, ALU.mult).then_inc(done, 1)

            def stats1(n):
                dve.wait_ge(s_x[n % 2], 16 * (n // 2 + 1))
                norm_stats(rows[:, n % 2, :], n, stats, mv, var, s_st1, s_mv1, s_var1)

            def norm1(n):
                if n >= 2:
                    dve.wait_ge(s_A1, n - 1)
                norm(normed[:, n % 2, :], rows[:, n % 2, :], n, mv, rstd, s_rs1, s_n1)

            stats1(0)
            norm1(0)
            dve.wait_ge(s_ids, 16)
            link(dve.tensor_copy(idf[:, :], ids[:, :]))
            for e in range(1, CE):
                last = dve.tensor_scalar(ge[:, e, :], idf[:, :], float(e * VSTEP), None, ALU.is_ge)
            link(last)
            mt = mine[:, :, :].rearrange("p t e -> p e t")
            dve.tensor_scalar(mt[:, 0, :], ge[:, 1, :], -1.0, 1.0, ALU.mult, ALU.add)
            dve.tensor_tensor(mt[:, 1:CE - 1, :], ge[:, 1:CE - 1, :], ge[:, 2:CE, :], ALU.subtract)
            dve.tensor_copy(mt[:, CE - 1, :], ge[:, CE - 1, :]).then_inc(s_mine, 1)
            dve.wait_ge(s_const, N_CONST)
            link(dve.tensor_scalar(ident[:, :], iota[:, :], part[:, 0:1], None, ALU.is_equal))
            dve.tensor_scalar(below[:, :], iota[:, :], part[:, 0:1], None, ALU.is_gt).then_inc(s_eye, 1)
            for k in range(KD):
                dve.wait_ge(s_ctxhi, k + 1)
                dve.tensor_tensor(ctx_lo[:, k, :], stage[:, k * CE * D:(k + 1) * CE * D],
                                  ctx_hi[:, k, :].bitcast(fp32), ALU.subtract).then_inc(s_ctxlo, 1)
            dve.wait_ge(s_mine, 1)

            def pick(out, src4, n, start, after, done_part, done):
                for e in range(start, CE):
                    at_ = src4[:, e // 2, (e % 2) * D:(e % 2 + 1) * D]
                    dve.scalar_tensor_tensor(out, at_, mine[:, n, e:e + 1], out, ALU.mult, ALU.add)\
                       .then_inc(done if e == CE - 1 else done_part, 1)
                    if e < CE - 1:
                        dve.wait_ge(done_part, n * (CE - 1 - start) + e - start + 1)

            for i in range(-1, TT + 3):
                a, b, c, d = i + 1, i, i - 1, i - 2
                if 0 <= c < TT:
                    dve.wait_ge(s_hhi1, c + 1)
                    dve.tensor_tensor(hidT_lo[:, c % 2, 0:D], ps_hid[:, 0:D], hidT_hi[:, c % 2, 0:D].bitcast(fp32),
                                      ALU.subtract).then_inc(s_hlo1, 1)
                if 0 <= d < TT:
                    dve.wait_ge(s_D1, d + 1)
                    dve.wait_ge(s_xres[d % 2], 16 * (d // 2 + 1))
                    pick(x2[:, d % 2, :], ps_y4, d, 0, None, s_x2p, s_x2)
                    dve.wait_ge(s_x2, d + 1)
                    norm_stats(x2[:, d % 2, :], d, stats2, mv2, var2, s_st2, s_mv2, s_var2)
                if 0 <= a + 1 < TT:
                    stats1(a + 1)
                if 0 <= b < TT:
                    dve.wait_ge(s_pick0, b + 1)
                    pick(picked[:, :], ps_up[0], b, 1, None, s_pickp, s_pick)
                if 0 <= a < TT:
                    dve.wait_ge(s_hi1, a + 1)
                    dve.tensor_tensor(inT_lo[:, a % 2, :], ps_in[:, 0:D], inT_hi[:, a % 2, :].bitcast(fp32),
                                      ALU.subtract).then_inc(s_lo1, 1)
                if 0 <= d < TT:
                    if d >= 2:
                        dve.wait_ge(s_stored[d % 2], 32 * (d // 2))
                    norm(h2[:, d % 2, :], x2[:, d % 2, :], d, mv2, rstd2, s_rs2, s_h2)
                if 0 <= b < TT:
                    dve.wait_ge(s_silu1, b + 1)
                    dve.tensor_tensor(hid[:, b % 2, 0:D], silu[:, 0:D], picked[:, :], ALU.mult).then_inc(s_hid1, 1)
                if 0 <= a + 1 < TT:
                    norm1(a + 1)
                if 0 <= i - 3 < TT:
                    dve.wait_ge(s_F1, i - 2)
                    dve.tensor_copy(lg[:, i - 3, :], ps_r[:, 0:E]).then_inc(s_lg, 1)

            def wide(x, shape):
                return x.to_broadcast(shape)

            def all_e(x):
                return x.unsqueeze(2).to_broadcast([P, TT, E])

            def over_t(x):
                return x.unsqueeze(1).to_broadcast([P, TT, E])

            def top(k, of):
                link(dve.tensor_reduce(m[:, k, :], of[:, :, :], AX, ALU.max))
                link(dve.tensor_tensor(eq[:, :, :], of[:, :, :], all_e(m[:, k, :]), ALU.is_equal))
                link(dve.tensor_tensor(wq[:, :, :], eq[:, :, :], over_t(rev[:, :]), ALU.mult))
                link(dve.tensor_reduce(best[:, :], wq[:, :, :], AX, ALU.max))
                link(dve.tensor_tensor(oh[:, k, :, :], wq[:, :, :], all_e(best[:, :]), ALU.is_equal))

            def choose():
                dve.wait_ge(s_lg, TT)
                top(0, lg)
                link(dve.scalar_tensor_tensor(lgx[:, :, :], oh[:, 0, :, :], -BIG, lg[:, :, :], ALU.mult, ALU.add))
                dve.tensor_tensor(sm[:, :, :], lg[:, :, :], all_e(m[:, 0, :]), ALU.subtract).then_inc(s_sm, 1)
                top(1, lgx)
                dve.tensor_tensor(taken[:, 0:TT, :], oh[:, 0, :, :], oh[:, 1, :, :], ALU.add).then_inc(s_taken, 1)

            def gates():
                dve.wait_ge(s_exp, 1)
                link(dve.tensor_reduce(ssum[:, :], sm[:, :, :], AX, ALU.add))
                link(dve.reciprocal(ssum[:, :], ssum[:, :]))
                link(dve.tensor_tensor(sm[:, :, :], sm[:, :, :], all_e(ssum[:, :]), ALU.mult))
                for k in range(TOPK):
                    last = dve.tensor_tensor(tpx[:, k, :, :], sm[:, :, :], oh[:, k, :, :], ALU.mult)
                link(last)
                link(dve.tensor_reduce(tp[:, :, :], tpx[:, :, :, :], AX, ALU.add))
                link(dve.tensor_tensor(ssum[:, :], tp[:, 0, :], tp[:, 1, :], ALU.add))
                link(dve.reciprocal(ssum[:, :], ssum[:, :]))
                link(dve.tensor_tensor(gate[:, :, :], tp[:, :, :], ssum[:, :].unsqueeze(1).to_broadcast([P, TOPK, TT]),
                                       ALU.mult))

            def places():
                dve.wait_ge(s_rank, 1)
                count = ps_r[:, TT * E:(TT + 1) * E]
                rank = ps_r[:, 0:TT * E].rearrange("p (t e) -> p t e", t=TT)
                link(dve.tensor_tensor(cmpk[:, :, :], count.unsqueeze(2).to_broadcast([P, E, TT]), k128[:, :, :],
                                       ALU.is_gt))
                link(dve.tensor_reduce(ntl[:, :], cmpk[:, :, :], AX, ALU.add))
                link(dve.tensor_tensor_scan(fend[:, :], ones8[:, :], ntl[:, :], 0.0, ALU.mult, ALU.add))
                link(dve.tensor_tensor(base[:, :], fend[:, :], ntl[:, :], ALU.subtract))
                link(dve.tensor_scalar(base[:, :], base[:, :], float(P), None, ALU.mult))
                link(dve.tensor_tensor(slot_e[:, :, :], rank, over_t(base[:, :]), ALU.add))
                link(dve.tensor_tensor(tpx[:, :, :, :], oh[:, :, :, :],
                                       slot_e[:, :, :].unsqueeze(1).to_broadcast([P, TOPK, TT, E]), ALU.mult))
                link(dve.tensor_reduce(pos[:, :, :], tpx[:, :, :, :], AX, ALU.add))
                link(dve.tensor_copy(posi[:, :], pos[:, :, :].rearrange("p k t -> p (k t)")))
                dve.tensor_scalar(loi[:, :], posi[:, :], P - 1, None, ALU.bitwise_and)
                link(dve.tensor_scalar(hii[:, :], posi[:, :], P.bit_length() - 1, None, ALU.logical_shift_right))
                dve.tensor_copy(lof[:, :], loi[:, :])
                link(dve.tensor_copy(hif[:, :], hii[:, :]))
                link(dve.tensor_tensor(cmpj[:, :, :], fend[:, :].unsqueeze(1).to_broadcast([P, RT, E]),
                                       jtile[:, :, :], ALU.is_le))
                link(dve.tensor_reduce(tef[:, :], cmpj[:, :, :], AX, ALU.add))
                dve.tensor_scalar(te[:, :], tef[:, :], float(E - 1), 1.0, ALU.min, ALU.add).then_inc(s_te, 1)

            def lists():
                C = TOPK * TT
                dve.wait_ge(s_ulo, (E + 1) * UNITS)
                link(dve.tensor_tensor(vals[:, :, 1, :], hif[:, :].unsqueeze(2).to_broadcast([P, C, RT]),
                                       iota[:, 0:RT].unsqueeze(1).to_broadcast([P, C, RT]), ALU.is_equal))
                for k in range(TOPK):
                    last = dve.tensor_tensor(vals[:, k * TT:(k + 1) * TT, 0, :], vals[:, k * TT:(k + 1) * TT, 1, :],
                                             tok1[:, :].unsqueeze(2).to_broadcast([P, TT, RT]), ALU.mult)
                link(last)
                dve.tensor_tensor(vals[:, :, 1, :], vals[:, :, 1, :],
                                  gate[:, :, :].rearrange("p k t -> p (k t)").unsqueeze(2).to_broadcast([P, C, RT]),
                                  ALU.mult).then_inc(s_vals, 1)
                for c in range(C):
                    if c >= 4:
                        dve.wait_ge(s_inv, c - 3)
                    dve.tensor_scalar(looh[:, c % 4, :], iota[:, :], lof[:, c:c + 1], None,
                                      ALU.is_equal).then_inc(s_looh, 1)

            def slots():
                C = TOPK * TT
                dve.wait_ge(s_inv, C)
                tok = ps_r[:, 128:128 + RT]
                dve.tensor_scalar(src[:, :], tok, -1.0, 0.0, ALU.add, ALU.max).then_inc(s_slots, 1)
                link(dve.tensor_scalar(used[:, :], tok, 1.0, None, ALU.min))
                link(dve.tensor_scalar(off[:, :], used[:, :], ntrash[:, 0:1], trash[:, 0:1], ALU.mult, ALU.add))
                dve.tensor_tensor(dst[:, :], tok, off[:, :], ALU.add).then_inc(s_slots, 1)
                link(dve.tensor_copy(sgate[:, :], ps_r[:, 128 + RT:128 + 2 * RT]))

            def ffn(at, shared=None):
                if j := at(-1):
                    dve.wait_ge(s_hhi, j.n + 1)
                    dve.tensor_tensor(hidT_lo[:, j.p, :], ps_hid[:, 0:NHC * P], hidT_hi[:, j.p, :].bitcast(fp32),
                                      ALU.subtract).then_inc(s_hlo, 1)
                if j := at(1):
                    dve.wait_ge(s_hi, j.n + 1)
                    dve.tensor_tensor(inT_lo[:, j.p, :], ps_in[:, 0:D], inT_hi[:, j.p, :].bitcast(fp32),
                                      ALU.subtract).then_inc(s_lo, 1)
                if j := at(-2):
                    dve.wait_ge(s_D, j.n + 1)
                    if shared:
                        dve.wait_ge(s_res[j.p], 16 * (j.before + 1))
                        if j.n >= 2:
                            dve.wait_ge(s_init[j.p], 16 * j.before)
                        dve.tensor_tensor(y_sb[:, j.p, :], ps_y[:, 0:D], x2[:, j.p, :], ALU.add).then_inc(s_y, 1)
                    else:
                        r = j.n - TT
                        if isinstance(r, int) and r < 2:
                            dve.wait_ge(s_init[j.p], 16 * (TT // 2))
                        else:
                            dve.wait_ge(s_added, 16 * (r - 1))
                        dve.tensor_scalar(y_sb[:, j.p, :], ps_y[:, 0:D], sgate[:, bass.ds(r, 1)], None,
                                          ALU.mult).then_inc(s_y, 1)
                if j := at(0):
                    dve.wait_ge(s_silu, j.n + 1)
                    dve.tensor_tensor(hid[:, j.p, 0:HP], silu[:, :], ps_up[j.p][:, 1, 0:HP], ALU.mult).then_inc(s_hid, 1)

            choose()
            gates()
            for i in range(-1, TT + 2):
                def at(k, i=i):
                    n = i + k
                    return Tile(n, n % 2, n // 2) if 0 <= n < NT else None
                ffn(at, shared=i - 2 < TT)
                {-1: places, 0: lists, 1: slots}.get(i, lambda: None)()
            pipeline(dve, TT + 2, TT + 4, NT - 1, NT + 2, NT, ffn)

        @block.tensor
        def _(pe):
            def products(out, terms, done):
                n = len(terms) * 3
                q = 0
                for (ah, al), (bh, bl) in terms:
                    for a, b in ((ah, bh), (ah, bl), (al, bh)):
                        last = pe.matmul(out, a, b, start=q == 0, stop=q == n - 1)
                        q += 1
                if done is not None:
                    last.then_inc(done, 1)

            def transposes(out, of, starts, done):
                for c, at_ in enumerate(starts):
                    last = pe.transpose(out[:, c * P:(c + 1) * P], of[:, at_:at_ + P], ident[:, :])
                last.then_inc(done, 1)

            def both(hi, lo, p, k):
                return hi[:, p, k * P:(k + 1) * P], lo[:, p, k * P:(k + 1) * P]

            def four(out, hi, lo, p, done):
                for b in range(2):
                    cols = slice(b * 2 * D, (b + 1) * 2 * D)
                    terms = [(both(hi, lo, p, k), (ctx_hi[:, k, cols], ctx_lo[:, k, cols])) for k in range(KD)]
                    products(out[:, b, :], terms, done if b else None)

            pe.wait_ge(s_eye, 1)
            for i in range(-1, TT + 3):
                a, b, c, d = i + 1, i, i - 1, i - 1
                if 0 <= c < TT:
                    pe.wait_ge(s_hid1, c + 1)
                    if c:
                        pe.wait_ge(s_hlo1, c)
                    transposes(ps_hid, hid[:, c % 2, :], range(0, D, P), s_C1)
                if 0 <= b < TT:
                    pe.wait_ge(s_lo1, b + 1)
                    if b == 0:
                        pe.wait_ge(s_ctxlo, KD)
                    else:
                        pe.wait_ge(s_pick, b)
                    four(ps_up[0], inT_hi, inT_lo, b % 2, s_B1)
                if 0 <= a < TT:
                    pe.wait_ge(s_n1, a + 1)
                    if a:
                        pe.wait_ge(s_lo1, a)
                    transposes(ps_in, normed[:, a % 2, :], range(0, D, P), s_A1)
                if 0 <= i - 3 < TT:
                    if i == 3:
                        pe.wait_ge(s_wr, 16)
                    else:
                        pe.wait_ge(s_lg, i - 3)
                    pe.wait_ge(s_h2T, i - 2)
                    for k in range(KD):
                        last = pe.matmul(ps_r[:, 0:E], h2T[:, k * P:(k + 1) * P], wr_sb[:, k, :], start=k == 0,
                                         stop=k == KD - 1)
                    last.then_inc(s_F1, 1)
                if 0 <= d < TT:
                    pe.wait_ge(s_hlo1, d + 1)
                    if d:
                        pe.wait_ge(s_x2, d)
                    four(ps_y4, hidT_hi, hidT_lo, d % 2, s_D1)
                if 0 <= i - 2 < TT:
                    pe.wait_ge(s_h2, i - 1)
                    if i > 2:
                        pe.wait_ge(s_h2T, i - 2)
                    transposes(ps_y, h2[:, i % 2, :], range(0, D, P), s_E1)

            def rank():
                pe.wait_ge(s_taken, 1)
                pe.wait_ge(s_lg, TT)
                out = ps_r[:, 0:(TT + 1) * E].rearrange("p (t e) -> p t e", e=E)
                pe.matmul(out, below[:, :], taken[:, :, :], start=True, stop=False)
                for t in range(TT):
                    n = TT - t
                    last = pe.matmul(out[:, t + 1:, :], ones[:, :],
                                     taken[:, t, :].unsqueeze(1).to_broadcast([P, n, E]),
                                     start=False, stop=t == TT - 1)
                last.then_inc(s_rank, 1)

            def invert():
                C = TOPK * TT
                pe.wait_ge(s_vals, 1)
                for c in range(C):
                    pe.wait_ge(s_looh, c + 1)
                    pe.matmul(ps_r[:, 128:128 + 2 * RT], looh[:, c % 4, :],
                              vals[:, c, :, :].rearrange("p v r -> p (v r)"),
                              start=c == 0, stop=c == C - 1).then_inc(s_inv, 1)

            def expert(j):
                if isinstance(j.n, int) and j.n < TT:
                    return 0
                return pe.value_load(te[0:1, bass.ds(j.n - TT, 1)], min_val=1, max_val=E)

            def ffn(at, shared=None):
                if j := at(0):
                    e = 0 if shared else expert(j)
                    pe.wait_ge(s_lo, j.n + 1)
                    if not (isinstance(j.n, int) and j.n < 2):
                        pe.wait_ge(s_hid, j.n - 1)
                    for half in range(2):
                        terms = [(both(inT_hi, inT_lo, j.p, k),
                                  tuple(w[:, e, k * U1 + half * HP:k * U1 + (half + 1) * HP] for w in (w13_hi, w13_lo)))
                                 for k in range(KD)]
                        products(ps_up[j.p][:, half, 0:HP], terms, s_B if half else None)
                if j := at(-1):
                    pe.wait_ge(s_hid, j.n + 1)
                    if not (isinstance(j.n, int) and j.n == 0):
                        pe.wait_ge(s_hlo, j.n)
                    transposes(ps_hid, hid[:, j.p, :], HC, s_C)
                if j := at(1):
                    rows_ready(j)
                    if not (isinstance(j.n, int) and j.n == 0):
                        pe.wait_ge(s_lo, j.n)
                    transposes(ps_in, rows[:, j.p, :], range(0, D, P), s_A)
                if j := at(-2):
                    e = 0 if shared or (isinstance(j.n, int) and j.n < TT) else expert(j)
                    pe.wait_ge(s_hlo, j.n + 1)
                    if not (isinstance(j.n, int) and j.n == 0):
                        pe.wait_ge(s_y, j.n)
                    terms = [(both(hidT_hi, hidT_lo, j.p, c),
                              tuple(w[:, e, c * D:(c + 1) * D] for w in (w2_hi, w2_lo))) for c in range(NHC)]
                    products(ps_y[:, 0:D], terms, s_D)

            def rows_ready(j):
                if isinstance(j.n, int) and j.n < TT:
                    pe.wait_ge(s_rows[j.p], 16 * (j.before + 1))
                else:
                    pe.wait_ge(s_gath[j.p], 16 * (j.before - TT // 2 + 1))

            pe.wait_ge(s_ulo, UNITS)
            rank()
            for i in range(-1, TT + 2):
                def at(k, i=i):
                    n = i + k
                    return Tile(n, n % 2, n // 2) if 0 <= n < NT else None
                if i == TT:
                    pe.wait_ge(s_te, 1)
                    pe.wait_ge(s_ulo, (E + 1) * UNITS)
                if i == 0:
                    pe.wait_ge(s_x2, TT)
                ffn(at)
                if i == 1:
                    invert()
            pipeline(pe, TT + 2, TT + 2, NT - 1, NT + 2, NT, ffn)


def kernel(x, itok_BxS_13_99985, ctx_2048, L0_ffn_sw1, L0_ffn_sw2, L0_ffn_sw3, L0_ffn_ew1, L0_ffn_ew2, L0_ffn_ew3,
           L0_ffn_wr):
    import concourse.bacc as bacc
    import numpy as np
    from concourse.bass_utils import run_bass_kernel_spmd

    def arr(a):
        return np.ascontiguousarray(np.asarray(a))

    x, ctx = arr(x), arr(ctx_2048)
    ids = arr(itok_BxS_13_99985)
    w1 = np.concatenate([arr(L0_ffn_sw1)[None], arr(L0_ffn_ew1)])
    w3 = np.concatenate([arr(L0_ffn_sw3)[None], arr(L0_ffn_ew3)])
    w2 = np.concatenate([arr(L0_ffn_sw2)[None], arr(L0_ffn_ew2)])
    arrays = {
        "x": x.reshape(T, D),
        "ids": arr(ids.reshape(TT, P).T),
        "ctx": arr(ctx.transpose(2, 0, 1).reshape(D, CE * D)),
        "w13": arr(np.stack([w1, w3], 1).transpose(0, 3, 1, 2)),
        "w2": arr(w2.transpose(0, 2, 1)),
        "wr": arr(arr(L0_ffn_wr).T),
    }
    nc = bacc.Bacc("TRN2", target_bir_lowering=False, num_devices=1)
    aps = [nc.dram_tensor("in_" + n, a.shape, mybir.dt.from_np(a.dtype), kind="ExternalInput").ap() for n, a in arrays.items()]
    out = nc.dram_tensor("out", (T, D), fp32, kind="ExternalOutput").ap()
    build(nc, *aps, out)
    r = run_bass_kernel_spmd(nc, [{"in_" + n: a for n, a in arrays.items()}], core_ids=[0])
    return r.results[0]["out"].reshape(x.shape)
```

```python
from collections import namedtuple
from contextlib import ExitStack

import concourse.bass as bass
from concourse import mybir

P = 128
T = 1024
D = 256
KD = D // P
TT = T // P
CE = 4
VOCAB = 12500
VSTEP = VOCAB // CE
E = 8
TOPK = 2
H = D * 4 // 3
HP = H + H % 2
NHC = -(-H // P)
HC = [min(c * P, H - P) for c in range(NHC)]
LAST = H - (NHC - 1) * P
RT = (TOPK * T + E * (P - 1)) // P
NT = TT + RT
NX = 3
EPS = 1e-5
U1 = 2 * HP
UNITS = KD + 1
UNIT_AT = [u * U1 for u in range(UNITS)] + [KD * U1 + NHC * D]
BIG = 3.0e38

fp32 = mybir.dt.float32
f32r = mybir.dt.float32r
bf16 = mybir.dt.bfloat16
i32 = mybir.dt.int32
u32 = mybir.dt.uint32
ALU = mybir.AluOpType
ACT = mybir.ActivationFunctionType
AX = mybir.AxisListType.X

Tile = namedtuple("Tile", "n p before")


def tile(g, c):
    return Tile(g * 2 + c, c % 2, g + c // 2)


def build(nc, x_d, ids_d, ctx_d, w13_d, w2_d, wr_d, out_d):
    es = ExitStack()
    with es:
        def sb(name, shape, dt=fp32):
            return es.enter_context(nc.sbuf_tensor(name, shape, dt))

        def sem(name):
            return es.enter_context(nc.semaphore(name))

        x2_dram = nc.dram_tensor("x2_rows", (T, D), fp32).ap()
        h2_dram = nc.dram_tensor("h2_rows", (T, D), fp32).ap()
        acc_dram = nc.dram_tensor("acc_rows", (T + P, D), fp32).ap()

        ctx_hi = sb("ctx_hi", [P, KD, CE * D], f32r)
        ctx_lo = sb("ctx_lo", [P, KD, CE * D], f32r)
        w13_hi = sb("w13_hi", [P, E + 1, KD * U1], f32r)
        w13_lo = sb("w13_lo", [P, E + 1, KD * U1], f32r)
        w2_hi = sb("w2_hi", [P, E + 1, NHC * D], f32r)
        w2_lo = sb("w2_lo", [P, E + 1, NHC * D], f32r)
        stage = sb("stage", [P, UNIT_AT[-1]])
        wr_sb = sb("wr_sb", [P, KD, E])

        rows = sb("rows", [P, 2, D])
        normed = sb("normed", [P, 2, D])
        inT_hi = sb("inT_hi", [P, 2, D], f32r)
        inT_lo = sb("inT_lo", [P, 2, D], f32r)
        picked = sb("picked", [P, D])
        silu = sb("silu", [P, HP])
        hid = sb("hid", [P, 2, HP])
        hidT_hi = sb("hidT_hi", [P, 2, NHC * P], f32r)
        hidT_lo = sb("hidT_lo", [P, 2, NHC * P], f32r)
        x2 = sb("x2", [P, NX, D])
        h2 = sb("h2", [P, 2, D])
        h2T = sb("h2T", [P, D])
        y_sb = normed
        stats = sb("stats", [P, 2, 6])
        mv = sb("mv", [P, 2, 2])
        rstd = sb("rstd", [P, 2, 2])
        stats2 = sb("stats2", [P, 2, 6])
        mv2 = sb("mv2", [P, 2, 2])
        minus_half = sb("minus_half", [P, 2])
        var = sb("var", [P, 2, 2])
        warm = sb("warm", [P, 1])
        N_CONST = 11

        ids = sb("ids", [P, TT], i32)
        idf = sb("idf", [P, TT])
        ge = sb("ge", [P, CE + 1, TT])
        mine = sb("mine", [P, TT, CE])
        iota = sb("iota", [P, P])
        part = sb("part", [P, 1])
        trash = sb("trash", [P, 1])
        ntrash = sb("ntrash", [P, 1])
        tok1 = sb("tok1", [P, TT])
        k128 = sb("k128", [P, E, TT])
        rev = sb("rev", [P, E])
        ident = sb("ident", [P, P])
        below = sb("below", [P, P], bf16)
        ones = sb("ones", [P, P], bf16)
        ones8 = sb("ones8", [P, E])
        lg = sb("lg", [P, TT, E])
        lgx = sb("lgx", [P, TT, E])
        m = sb("m", [P, TOPK, TT])
        eq = sb("eq", [P, TT, E])
        wq = sb("wq", [P, TT, E])
        best = sb("best", [P, TT])
        oh = sb("oh", [P, TOPK, TT, E])
        taken = sb("taken", [P, TT + 1, E], bf16)
        sm = sb("sm", [P, TT, E])
        ssum = sb("ssum", [P, TT])
        tp = sb("tp", [P, TOPK, TT])
        gate = sb("gate", [P, TOPK, TT])
        tpx = sb("tpx", [P, TOPK, TT, E])
        cmpk = sb("cmpk", [P, E, TT])
        ntl = sb("ntl", [P, E])
        fend = sb("fend", [P, E])
        base = sb("base", [P, E])
        slot_e = sb("slot_e", [P, TT, E])
        pos = sb("pos", [P, TOPK, TT])
        posi = sb("posi", [P, TOPK * TT], i32)
        loi = sb("loi", [P, TOPK * TT], i32)
        hii = sb("hii", [P, TOPK * TT], i32)
        lof = sb("lof", [P, TOPK * TT])
        hif = sb("hif", [P, TOPK * TT])
        cmpj = sb("cmpj", [P, RT, E])
        tef = sb("tef", [P, RT])
        te = sb("te", [P, RT], i32)
        vals = stage[:, 0:TOPK * TT * 2 * RT].rearrange("p (c v r) -> p c v r", c=TOPK * TT, v=2)
        looh = ctx_hi[:, :, :].rearrange("p k (c n) -> p (k c) n", n=P)
        used = sb("used", [P, RT])
        off = sb("off", [P, RT])
        src = sb("src", [P, RT], u32)
        dst = sb("dst", [P, RT], u32)
        sgate = sb("sgate", [P, RT])

        ps = es.enter_context(nc.psum_tensor("ps", [P, 8, 512], fp32))
        ps_in = ps[:, 0, :]
        ps_up = [ps[:, 1:3, :], ps[:, 3:5, :]]
        ps_y4 = ps[:, 3:5, :]
        ps_hid = ps[:, 5, :]
        ps_y = ps[:, 6, :]
        ps_r = ps[:, 7, :]

        s_ctx = [sem(f"ctx_loaded{k}") for k in range(KD)]
        s_wr, s_ids = sem("wr_loaded"), sem("ids_loaded")
        s_ctxhi, s_ctxlo = sem("ctx_hi_done"), sem("ctx_lo_done")
        s_const, s_eye, s_pad = sem("constants"), sem("matrices_made"), sem("pads_zeroed")
        s_unit = [sem(f"unit_loaded{u}") for u in range(UNITS)]
        s_uhi, s_ulo = sem("unit_hi_done"), sem("unit_lo_done")
        s_idf, s_ge, s_mine = sem("idf"), sem("ge"), sem("mine")
        s_x = [sem("x_loaded0"), sem("x_loaded1")]
        s_xres = [sem(f"x_residual_loaded{b}") for b in range(NX)]
        s_var1, s_var2 = sem("var1"), sem("var2")
        s_pick0, s_pickp, s_x2p = sem("picked0"), sem("picked_part"), sem("x2_part")
        s_st1, s_mv1, s_rs, s_n1 = sem("stats1"), sem("mv1"), sem("rstd"), sem("normed1")
        s_A1, s_hi1, s_lo1 = sem("in_transposed1"), sem("inT_hi1"), sem("inT_lo1")
        s_B1, s_pick, s_silu1, s_hid1 = sem("up1"), sem("picked"), sem("silu1"), sem("hid1")
        s_C1, s_hhi1, s_hlo1 = sem("hid_transposed1"), sem("hidT_hi1"), sem("hidT_lo1")
        s_D1, s_acc1, s_x2 = sem("down1"), sem("x2_partial"), sem("x2_ready")
        s_st2, s_mv2, s_h2 = sem("stats2"), sem("mv2"), sem("h2_ready")
        s_E1, s_h2T, s_F1, s_lg = sem("h2_transposed"), sem("h2T_copied"), sem("logits"), sem("logits_copied")
        s_x2st = [sem(f"x2_stored{b}") for b in range(NX)]
        s_h2st = [sem("h2_stored0"), sem("h2_stored1")]

        s_rows = [sem("rows_loaded0"), sem("rows_loaded1")]
        s_res = [sem("residual_loaded0"), sem("residual_loaded1")]
        s_gath = [sem("rows_gathered0"), sem("rows_gathered1")]
        s_A, s_hi, s_lo = sem("in_transposed"), sem("inT_hi_done"), sem("inT_lo_done")
        s_B, s_silu, s_hid = sem("up_done"), sem("silu_done"), sem("hid_done")
        s_C, s_hhi, s_hlo = sem("hid_transposed"), sem("hidT_hi_done"), sem("hidT_lo_done")
        s_D, s_y = sem("down_done"), sem("y_ready")
        s_init = [sem("acc_written0"), sem("acc_written1")]
        s_added = sem("acc_added")

        s_dv = sem("vector_routing_step")
        s_taken, s_rank, s_te = sem("taken"), sem("ranked"), sem("tile_experts")
        s_sm, s_exp = sem("softmax_shifted"), sem("softmax_exp")
        s_lof = sem("places_known")
        s_vals, s_looh, s_inv = sem("vals"), sem("lo_onehot"), sem("lo_onehot_used")
        s_slots, s_fin = sem("slots_ready"), sem("out_written")
        block = es.enter_context(nc.Block())


        def unit(u, part_, e):
            return part_[0][:, e, u * U1:(u + 1) * U1] if u < KD else part_[1][:, e, :]

        def pipeline(eng, first, lo, hi, end, count, step):
            def peeled(i):
                def at(k):
                    n = i + k
                    return Tile(n, n % 2, n // 2) if 0 <= n < count else None
                step(at)
            for i in range(first, lo):
                peeled(i)
            if hi > lo:
                with eng.Fori(lo // 2, hi // 2) as g:
                    for c in (0, 1):
                        step(lambda k: tile(g, c + k))
            for i in range(hi, end):
                peeled(i)

        HI, LO = (w13_hi, w2_hi), (w13_lo, w2_lo)

        @block.sync
        def _(sp):
            def load_expert(e):
                for u in range(UNITS):
                    if e > 0:
                        sp.wait_ge(s_ulo, (e - 1) * UNITS + u + 1)
                    if u < KD:
                        to = stage[:, UNIT_AT[u]:UNIT_AT[u + 1]].rearrange("p (a h) -> p a h", a=2)
                        sp.dma_start(to[:, :, 0:H], w13_d[e, u * P:(u + 1) * P, :, :]).then_inc(s_unit[u], 16)
                    else:
                        to = stage[:, UNIT_AT[u]:UNIT_AT[u + 1]].rearrange("p (c d) -> p c d", c=NHC)
                        full = w2_d[e, 0:(NHC - 1) * P, :].rearrange("(c p) d -> p c d", p=P)
                        sp.dma_start(to[:, 0:NHC - 1, :], full).then_inc(s_unit[u], 16)
                        sp.dma_start(to[P - LAST:P, NHC - 1, :], w2_d[e, (NHC - 1) * P:H, :]).then_inc(s_unit[u], 16)

            def load_rows(j):
                sp.dma_start(rows[:, j.p, :], h2_dram[bass.ts(j.n, P), :]).then_inc(s_rows[j.p], 16)

            raw = stage[:, 0:KD * CE * D].rearrange("p (k n) -> p k n", k=KD)
            sp.dma_start(rows[:, 0, :], x_d[0:P, :]).then_inc(s_x[0], 16)
            for k in range(KD):
                sp.dma_start(raw[:, k, :], ctx_d[k * P:(k + 1) * P, :]).then_inc(s_ctx[k], 16)
            for n in range(NX):
                sp.dma_start(x2[:, n, :], x_d[bass.ts(n, P), :]).then_inc(s_xres[n], 16)
            sp.dma_start(wr_sb[:, :, :], wr_d.rearrange("(k p) e -> p k e", p=P)).then_inc(s_wr, 16)
            sp.wait_ge(s_ctxlo, KD)
            for e in range(E + 1):
                load_expert(e)
            sp.wait_ge(s_n1, TT)
            for p in (0, 1):
                sp.wait_ge(s_h2st[p], 16)
                load_rows(Tile(p, p, 0))

            def load_residual(j):
                sp.dma_start(x2[:, j.p, :], x2_dram[bass.ts(j.n, P), :]).then_inc(s_res[j.p], 16)

            def shared(at):
                if at(2):
                    sp.wait_ge(s_A, at(0).n + 1)
                    load_rows(at(2))
                if j := at(-2):
                    sp.wait_ge(s_y, j.n + 1)
                    sp.dma_start(acc_dram[bass.ts(j.n, P), :], y_sb[:, j.p, :]).then_inc(s_init[j.p], 16)
                    if at(0):
                        load_residual(at(0))

            for p in (0, 1):
                sp.wait_ge(s_h2st[p], 16 * (TT // 2))
            for b in range(NX):
                sp.wait_ge(s_x2st[b], 16 * len(range(b, TT, NX)))
            for p in (0, 1):
                load_residual(Tile(p, p, 0))
            pipeline(sp, 0, 2, TT - 2, TT + 2, TT, shared)
            sp.wait_ge(s_added, 16 * RT)
            sp.dma_start(out_d, acc_dram[0:T, :]).then_inc(s_fin, 16)
            sp.wait_ge(s_fin, 16)

        @block.gpsimd
        def _(pool):
            pool.memset(minus_half[:, :], -0.5).then_inc(s_const, 1)
            pool.memset(ones8[:, :], 1.0).then_inc(s_const, 1)
            pool.memset(ones[:, :], 1.0).then_inc(s_const, 1)
            pool.memset(taken[:, TT, :], 0.0).then_inc(s_const, 1)
            one = dict(allow_small_or_imprecise_dtypes=True)
            pool.iota(iota[:, :], [[1, P]], base=0, channel_multiplier=0, **one).then_inc(s_const, 1)
            pool.iota(part[:, :], [[1, 1]], base=0, channel_multiplier=1, **one).then_inc(s_const, 1)
            pool.iota(trash[:, :], [[1, 1]], base=T, channel_multiplier=1, **one).then_inc(s_const, 1)
            pool.iota(ntrash[:, :], [[1, 1]], base=-(T + 1), channel_multiplier=-1, **one).then_inc(s_const, 1)
            pool.iota(tok1[:, :], [[P, TT]], base=1, channel_multiplier=1, **one).then_inc(s_const, 1)
            pool.iota(k128[:, :, :], [[0, E], [P, TT]], base=0, channel_multiplier=0, **one).then_inc(s_const, 1)
            pool.iota(rev[:, :], [[-1, E]], base=E, channel_multiplier=0, **one).then_inc(s_const, 1)

            def low(n):
                e, u = divmod(n, UNITS)
                pool.wait_ge(s_uhi, n + 1)
                pool.tensor_tensor(unit(u, LO, e), stage[:, UNIT_AT[u]:UNIT_AT[u + 1]],
                                   unit(u, HI, e).bitcast(fp32), ALU.subtract).then_inc(s_ulo, 1)

            pool.wait_ge(s_const, 1)
            for i in range(-2, TT + 2):
                if i == 0:
                    pool.wait_ge(s_ctxlo, KD)
                    pads = stage[:, 0:KD * U1].rearrange("p (m h) -> p m h", h=HP)[:, :, H:HP]
                    pool.memset(pads, 0.0).then_inc(s_pad, 1)
                    pool.memset(stage[0:P - LAST, UNIT_AT[-1] - D:], 0.0).then_inc(s_pad, 1)
                cols = [c for c, n in ((0, i - 2), (1, i + 2)) if 0 <= n < TT]
                if 0 in cols:
                    pool.wait_ge(s_var2, i - 1)
                if 1 in cols:
                    pool.wait_ge(s_var1, i + 3)
                cut = slice(cols[0], cols[-1] + 1)
                pool.tensor_tensor(rstd[:, i % 2, cut], var[:, i % 2, cut], minus_half[:, 0:len(cols)],
                                   ALU.pow).then_inc(s_rs, 1)
                if 0 <= i <= E:
                    for u in range(UNITS):
                        low(i * UNITS + u)

            pool.wait_ge(s_lof, 1)
            for c in range(TOPK * TT):
                pool.tensor_scalar(looh[:, c, :], iota[:, :], lof[:, c:c + 1], None,
                                   ALU.is_equal).then_inc(s_looh, 1)

            pool.wait_ge(s_slots, 2)
            for r in range(-2, RT + 3):
                if r + 2 < RT:
                    n = r + 2
                    pool.wait_ge(s_A, n + TT - 1)
                    pool.indirect_dma_start(out=rows[:, n % 2, :], out_offset=None, in_=h2_dram,
                                            in_offset=bass.IndirectOffsetOnAxis(ap=src[:, n:n + 1], axis=0),
                                            ).then_inc(s_gath[n % 2], 16)
                if r - 3 >= 0:
                    n = r - 3
                    pool.wait_ge(s_y, n + TT + 1)
                    if n == 0:
                        for p in (0, 1):
                            pool.wait_ge(s_init[p], 16 * (TT // 2))
                    else:
                        pool.wait_ge(s_added, n * 16)
                    pool.indirect_dma_start(out=acc_dram, in_=y_sb[:, n % 2, :], in_offset=None,
                                            out_offset=bass.IndirectOffsetOnAxis(ap=dst[:, n:n + 1], axis=0),
                                            compute_op=ALU.add).then_inc(s_added, 16)

        @block.scalar
        def _(act):
            def load_x(t):
                act.dma_start(rows[:, t % 2, :], x_d[bass.ts(t, P), :]).then_inc(s_x[t % 2], 16)

            def high(n):
                e, u = divmod(n, UNITS)
                act.wait_ge(s_unit[u], (16 if u < KD else 32) * (e + 1))
                act.activation(unit(u, HI, e), stage[:, UNIT_AT[u]:UNIT_AT[u + 1]], ACT.Copy).then_inc(s_uhi, 1)

            act.dma_start(ids[:, :], ids_d).then_inc(s_ids, 16)
            load_x(1)
            raw = stage[:, 0:KD * CE * D].rearrange("p (k n) -> p k n", k=KD)
            for k in range(KD):
                act.wait_ge(s_ctx[k], 16)
                act.activation(ctx_hi[:, k, :], raw[:, k, :], ACT.Copy).then_inc(s_ctxhi, 1)
            def ffn(at):
                if j := at(0):
                    act.wait_ge(s_B, j.n + 1)
                    if not (isinstance(j.n, int) and j.n == 0):
                        act.wait_ge(s_hid, j.n)
                    act.activation(silu[:, :], ps_up[j.p][:, 0, 0:HP], ACT.Silu).then_inc(s_silu, 1)
                if j := at(1):
                    act.wait_ge(s_A, j.n + 1)
                    act.activation(inT_hi[:, j.p, :], ps_in[:, 0:D], ACT.Copy).then_inc(s_hi, 1)
                if j := at(-1):
                    act.wait_ge(s_C, j.n + 1)
                    act.activation(hidT_hi[:, j.p, :], ps_hid[:, 0:NHC * P], ACT.Copy).then_inc(s_hhi, 1)

            for i in range(-1, TT + 3):
                a, b, c, e = i + 1, i, i - 1, i - 3
                if 0 <= c < TT:
                    act.wait_ge(s_C1, c + 1)
                    act.activation(hidT_hi[:, c % 2, 0:D], ps_hid[:, 0:D], ACT.Copy).then_inc(s_hhi1, 1)
                if 0 <= e < TT:
                    act.wait_ge(s_h2, e + 1)
                    act.dma_start(h2_dram[bass.ts(e, P), :], h2[:, e % 2, :]).then_inc(s_h2st[e % 2], 16)
                    act.dma_start(x2_dram[bass.ts(e, P), :], x2[:, e % NX, :]).then_inc(s_x2st[e % NX], 16)
                if NX <= b - 1 < TT:
                    act.wait_ge(s_x2st[(b - 1) % NX], 16 * ((b - 1) // NX))
                    act.dma_start(x2[:, (b - 1) % NX, :], x_d[bass.ts(b - 1, P), :]).then_inc(s_xres[(b - 1) % NX], 16)
                if 0 <= i - 1 <= E:
                    high(i * UNITS - 1)
                if 0 <= b < TT:
                    act.wait_ge(s_B1, b + 1)
                    if b:
                        act.wait_ge(s_hid1, b)
                    act.activation(picked[:, :], ps_up[0][:, 0, 0:D], ACT.Copy,
                                   scale=mine[:, b, 0:1]).then_inc(s_pick0, 1)
                if 0 <= a < TT:
                    act.wait_ge(s_A1, a + 1)
                    act.activation(inT_hi[:, a % 2, :], ps_in[:, 0:D], ACT.Copy).then_inc(s_hi1, 1)
                    if a + 2 < TT:
                        load_x(a + 2)
                if i == TT + 2:
                    ffn(lambda k: Tile(0, 0, 0) if k == 1 else None)
                if 0 <= e < TT:
                    act.wait_ge(s_E1, e + 1)
                    if e:
                        act.wait_ge(s_F1, e)
                    act.activation(h2T[:, :], ps_y[:, 0:D], ACT.Copy).then_inc(s_h2T, 1)
                if i == 0:
                    act.wait_ge(s_pad, 2)
                if 0 <= i <= E:
                    high(i * UNITS)
                if 0 <= b < TT:
                    act.wait_ge(s_pick, b + 1)
                    act.activation(silu[:, 0:D], picked[:, :], ACT.Silu).then_inc(s_silu1, 1)
                if 0 <= i <= E:
                    for u in range(1, UNITS - 1):
                        high(i * UNITS + u)
            act.wait_ge(s_sm, 1)
            act.activation(sm[:, :, :], sm[:, :, :], ACT.Exp).then_inc(s_exp, 1)
            act.activation(warm[:, :], part[:, :], ACT.Silu)
            pipeline(act, 0, 2, NT - 1, NT + 1, NT, ffn)

        @block.vector
        def _(dve):
            steps = [0]

            def link(ins):
                steps[0] += 1
                ins.then_inc(s_dv, 1)
                dve.wait_ge(s_dv, steps[0])

            def stats1(n):
                p = n % 2
                dve.wait_ge(s_x[p], 16 * (n // 2 + 1))
                dve.bn_stats(stats[:, p, :], rows[:, p, :]).then_inc(s_st1, 1)
                yield
                dve.wait_ge(s_st1, n + 1)
                dve.bn_aggr(mv[:, p, :], stats[:, p, :]).then_inc(s_mv1, 1)
                yield
                dve.wait_ge(s_mv1, n + 1)
                dve.tensor_scalar(var[:, p, 1:2], mv[:, p, 1:2], EPS, None, ALU.add).then_inc(s_var1, 1)
                yield

            def stats_h2(n):
                p = n % 2
                dve.wait_ge(s_x2, n + 1)
                dve.bn_stats(stats2[:, p, :], x2[:, n % NX, :]).then_inc(s_st2, 1)
                yield
                dve.wait_ge(s_st2, n + 1)
                dve.bn_aggr(mv2[:, p, :], stats2[:, p, :]).then_inc(s_mv2, 1)
                yield
                dve.wait_ge(s_mv2, n + 1)
                dve.tensor_scalar(var[:, p, 0:1], mv2[:, p, 1:2], EPS, None, ALU.add).then_inc(s_var2, 1)
                yield

            def norm1(n):
                p = n % 2
                if n >= 2:
                    dve.wait_ge(s_A1, n - 1)
                dve.wait_ge(s_rs, n + 1)
                dve.tensor_scalar(normed[:, p, :], rows[:, p, :], mv[:, p, 0:1], rstd[:, p, 1:2], ALU.subtract,
                                  ALU.mult).then_inc(s_n1, 1)

            def norm_h2(n):
                p = n % 2
                if n >= 2:
                    dve.wait_ge(s_h2st[p], 16 * (n // 2))
                dve.wait_ge(s_rs, n + 5)
                dve.tensor_scalar(h2[:, p, :], x2[:, n % NX, :], mv2[:, p, 0:1], rstd[:, p, 0:1], ALU.subtract,
                                  ALU.mult).then_inc(s_h2, 1)

            def in_turn(*steps_):
                chains = [iter(x) for x in steps_]
                while chains:
                    for x in list(chains):
                        if next(x, "end") == "end":
                            chains.remove(x)

            dve.wait_ge(s_const, N_CONST)
            link(dve.tensor_scalar(ident[:, :], iota[:, :], part[:, 0:1], None, ALU.is_equal))
            dve.tensor_scalar(below[:, :], iota[:, :], part[:, 0:1], None, ALU.is_gt).then_inc(s_eye, 1)
            in_turn(stats1(0))
            dve.wait_ge(s_ids, 16)
            link(dve.tensor_copy(idf[:, :], ids[:, :]))
            for e in range(1, CE):
                last = dve.tensor_scalar(ge[:, e, :], idf[:, :], float(e * VSTEP), None, ALU.is_ge)
            link(last)
            mt = mine[:, :, :].rearrange("p t e -> p e t")
            dve.tensor_scalar(mt[:, 0, :], ge[:, 1, :], -1.0, 1.0, ALU.mult, ALU.add)
            dve.tensor_tensor(mt[:, 1:CE - 1, :], ge[:, 1:CE - 1, :], ge[:, 2:CE, :], ALU.subtract)
            dve.tensor_copy(mt[:, CE - 1, :], ge[:, CE - 1, :]).then_inc(s_mine, 1)
            norm1(0)

            def ctx_low(k):
                dve.wait_ge(s_ctxhi, k + 1)
                dve.tensor_tensor(ctx_lo[:, k, :], stage[:, k * CE * D:(k + 1) * CE * D],
                                  ctx_hi[:, k, :].bitcast(fp32), ALU.subtract).then_inc(s_ctxlo, 1)

            ctx_low(0)
            in_turn(stats1(1))
            dve.wait_ge(s_mine, 1)

            def pick(out, src4, n, start, done_part, done):
                for e in range(start, CE):
                    at_ = src4[:, e // 2, (e % 2) * D:(e % 2 + 1) * D]
                    dve.scalar_tensor_tensor(out, at_, mine[:, n, e:e + 1], out, ALU.mult, ALU.add)\
                       .then_inc(done if e == CE - 1 else done_part, 1)
                    yield
                    if e < CE - 1:
                        dve.wait_ge(done_part, n * (CE - 1 - start) + e - start + 1)

            def down(n):
                dve.wait_ge(s_D1, n + 1)
                dve.wait_ge(s_xres[n % NX], 16 * (n // NX + 1))
                return pick(x2[:, n % NX, :], ps_y4, n, 0, s_x2p, s_x2)

            def ffn(at, shared=None):
                if j := at(1):
                    dve.wait_ge(s_hi, j.n + 1)
                    dve.tensor_tensor(inT_lo[:, j.p, :], ps_in[:, 0:D], inT_hi[:, j.p, :].bitcast(fp32),
                                      ALU.subtract).then_inc(s_lo, 1)
                if j := at(-1):
                    dve.wait_ge(s_hhi, j.n + 1)
                    dve.tensor_tensor(hidT_lo[:, j.p, :], ps_hid[:, 0:NHC * P], hidT_hi[:, j.p, :].bitcast(fp32),
                                      ALU.subtract).then_inc(s_hlo, 1)
                if j := at(0):
                    dve.wait_ge(s_silu, j.n + 1)
                    dve.tensor_tensor(hid[:, j.p, 0:HP], silu[:, :], ps_up[j.p][:, 1, 0:HP], ALU.mult).then_inc(s_hid, 1)
                if j := at(-2):
                    dve.wait_ge(s_D, j.n + 1)
                    if shared:
                        dve.wait_ge(s_res[j.p], 16 * (j.before + 1))
                        if j.n >= 2:
                            dve.wait_ge(s_init[j.p], 16 * j.before)
                        dve.tensor_tensor(y_sb[:, j.p, :], ps_y[:, 0:D], x2[:, j.p, :], ALU.add).then_inc(s_y, 1)
                    else:
                        r = j.n - TT
                        if isinstance(r, int) and r < 2:
                            dve.wait_ge(s_init[j.p], 16 * (TT // 2))
                        else:
                            dve.wait_ge(s_added, 16 * (r - 1))
                        dve.tensor_scalar(y_sb[:, j.p, :], ps_y[:, 0:D], sgate[:, bass.ds(r, 1)], None,
                                          ALU.mult).then_inc(s_y, 1)

            for i in range(-1, TT + 4):
                a, b, c, d, n = i + 1, i, i - 1, i - 2, i + 2
                if 0 <= c < TT:
                    dve.wait_ge(s_hhi1, c + 1)
                    dve.tensor_tensor(hidT_lo[:, c % 2, 0:D], ps_hid[:, 0:D], hidT_hi[:, c % 2, 0:D].bitcast(fp32),
                                      ALU.subtract).then_inc(s_hlo1, 1)
                in_turn(down(d) if 0 <= d < TT else (), stats1(n) if 2 <= n < TT else ())
                if 0 <= b < TT:
                    dve.wait_ge(s_pick0, b + 1)
                in_turn(pick(picked[:, :], ps_up[0], b, 1, s_pickp, s_pick) if 0 <= b < TT else (),
                        stats_h2(d) if 0 <= d < TT else ())
                if 0 <= a < TT:
                    dve.wait_ge(s_hi1, a + 1)
                    dve.tensor_tensor(inT_lo[:, a % 2, :], ps_in[:, 0:D], inT_hi[:, a % 2, :].bitcast(fp32),
                                      ALU.subtract).then_inc(s_lo1, 1)
                if i == -1:
                    ctx_low(1)
                if 0 <= b < TT:
                    dve.wait_ge(s_silu1, b + 1)
                    dve.tensor_tensor(hid[:, b % 2, 0:D], silu[:, 0:D], picked[:, :], ALU.mult).then_inc(s_hid1, 1)
                if 0 <= d < TT:
                    norm_h2(d)
                if 0 <= n < TT:
                    norm1(n)
                if i == TT + 1:
                    ffn(lambda k: Tile(0, 0, 0) if k == 1 else None)
                if 0 <= i - 4 < TT:
                    dve.wait_ge(s_F1, i - 3)
                    dve.tensor_copy(lg[:, i - 4, :], ps_r[:, 0:E]).then_inc(s_lg, 1)

            def wide(x, shape):
                return x.to_broadcast(shape)

            def all_e(x):
                return x.unsqueeze(2).to_broadcast([P, TT, E])

            def over_t(x):
                return x.unsqueeze(1).to_broadcast([P, TT, E])

            def top(k, of):
                link(dve.tensor_reduce(m[:, k, :], of[:, :, :], AX, ALU.max))
                link(dve.tensor_tensor(eq[:, :, :], of[:, :, :], all_e(m[:, k, :]), ALU.is_equal))
                link(dve.tensor_tensor(wq[:, :, :], eq[:, :, :], over_t(rev[:, :]), ALU.mult))
                link(dve.tensor_reduce(best[:, :], wq[:, :, :], AX, ALU.max))
                link(dve.tensor_tensor(oh[:, k, :, :], wq[:, :, :], all_e(best[:, :]), ALU.is_equal))

            def choose():
                dve.wait_ge(s_lg, TT)
                top(0, lg)
                link(dve.scalar_tensor_tensor(lgx[:, :, :], oh[:, 0, :, :], -BIG, lg[:, :, :], ALU.mult, ALU.add))
                dve.tensor_tensor(sm[:, :, :], lg[:, :, :], all_e(m[:, 0, :]), ALU.subtract).then_inc(s_sm, 1)
                top(1, lgx)
                dve.tensor_tensor(taken[:, 0:TT, :], oh[:, 0, :, :], oh[:, 1, :, :], ALU.add).then_inc(s_taken, 1)

            def gates():
                dve.wait_ge(s_exp, 1)
                link(dve.tensor_reduce(ssum[:, :], sm[:, :, :], AX, ALU.add))
                link(dve.reciprocal(ssum[:, :], ssum[:, :]))
                link(dve.tensor_tensor(sm[:, :, :], sm[:, :, :], all_e(ssum[:, :]), ALU.mult))

            def gates2():
                for k in range(TOPK):
                    last = dve.tensor_tensor(tpx[:, k, :, :], sm[:, :, :], oh[:, k, :, :], ALU.mult)
                link(last)
                link(dve.tensor_reduce(tp[:, :, :], tpx[:, :, :, :], AX, ALU.add))
                link(dve.tensor_tensor(ssum[:, :], tp[:, 0, :], tp[:, 1, :], ALU.add))
                link(dve.reciprocal(ssum[:, :], ssum[:, :]))
                link(dve.tensor_tensor(gate[:, :, :], tp[:, :, :], ssum[:, :].unsqueeze(1).to_broadcast([P, TOPK, TT]),
                                       ALU.mult))

            def bases():
                dve.wait_ge(s_rank, 1)
                count = ps_r[:, TT * E:(TT + 1) * E]
                link(dve.tensor_tensor(cmpk[:, :, :], count.unsqueeze(2).to_broadcast([P, E, TT]), k128[:, :, :],
                                       ALU.is_gt))
                link(dve.tensor_reduce(ntl[:, :], cmpk[:, :, :], AX, ALU.add))
                link(dve.tensor_tensor_scan(fend[:, :], ones8[:, :], ntl[:, :], 0.0, ALU.mult, ALU.add))
                link(dve.tensor_tensor(base[:, :], fend[:, :], ntl[:, :], ALU.subtract))
                link(dve.tensor_scalar(base[:, :], base[:, :], float(P), None, ALU.mult))

            def places():
                rank = ps_r[:, 0:TT * E].rearrange("p (t e) -> p t e", t=TT)
                link(dve.tensor_tensor(slot_e[:, :, :], rank, over_t(base[:, :]), ALU.add))
                link(dve.tensor_tensor(tpx[:, :, :, :], oh[:, :, :, :],
                                       slot_e[:, :, :].unsqueeze(1).to_broadcast([P, TOPK, TT, E]), ALU.mult))
                link(dve.tensor_reduce(pos[:, :, :], tpx[:, :, :, :], AX, ALU.add))
                link(dve.tensor_copy(posi[:, :], pos[:, :, :].rearrange("p k t -> p (k t)")))
                dve.tensor_scalar(loi[:, :], posi[:, :], P - 1, None, ALU.bitwise_and)
                link(dve.tensor_scalar(hii[:, :], posi[:, :], P.bit_length() - 1, None, ALU.logical_shift_right))
                dve.tensor_copy(lof[:, :], loi[:, :])
                last = dve.tensor_copy(hif[:, :], hii[:, :])
                last.then_inc(s_lof, 1)
                dve.wait_ge(s_lof, 1)

            def tile_experts():
                link(dve.tensor_tensor(cmpj[:, :, :], fend[:, :].unsqueeze(1).to_broadcast([P, RT, E]),
                                       iota[:, 0:RT].unsqueeze(2).to_broadcast([P, RT, E]), ALU.is_le))
                link(dve.tensor_reduce(tef[:, :], cmpj[:, :, :], AX, ALU.add))
                dve.tensor_scalar(te[:, :], tef[:, :], float(E - 1), 1.0, ALU.min, ALU.add).then_inc(s_te, 1)

            def lists():
                C = TOPK * TT
                dve.wait_ge(s_ulo, (E + 1) * UNITS)
                link(dve.tensor_tensor(vals[:, :, 1, :], hif[:, :].unsqueeze(2).to_broadcast([P, C, RT]),
                                       iota[:, 0:RT].unsqueeze(1).to_broadcast([P, C, RT]), ALU.is_equal))
                for k in range(TOPK):
                    last = dve.tensor_tensor(vals[:, k * TT:(k + 1) * TT, 0, :], vals[:, k * TT:(k + 1) * TT, 1, :],
                                             tok1[:, :].unsqueeze(2).to_broadcast([P, TT, RT]), ALU.mult)
                link(last)
                dve.tensor_tensor(vals[:, :, 1, :], vals[:, :, 1, :],
                                  gate[:, :, :].rearrange("p k t -> p (k t)").unsqueeze(2).to_broadcast([P, C, RT]),
                                  ALU.mult).then_inc(s_vals, 1)

            def slots():
                C = TOPK * TT
                dve.wait_ge(s_inv, C)
                tok = ps_r[:, 128:128 + RT]
                dve.tensor_scalar(src[:, :], tok, -1.0, 0.0, ALU.add, ALU.max).then_inc(s_slots, 1)
                link(dve.tensor_scalar(used[:, :], tok, 1.0, None, ALU.min))
                link(dve.tensor_scalar(off[:, :], used[:, :], ntrash[:, 0:1], trash[:, 0:1], ALU.mult, ALU.add))
                dve.tensor_tensor(dst[:, :], tok, off[:, :], ALU.add).then_inc(s_slots, 1)
                link(dve.tensor_copy(sgate[:, :], ps_r[:, 128 + RT:128 + 2 * RT]))

            choose()
            bases()
            turns = {0: [places, gates], 1: [gates2, lists], 2: [tile_experts], 3: [slots]}
            for i in range(0, TT + 2):
                def at(k, i=i):
                    n = i + k
                    return Tile(n, n % 2, n // 2) if 0 <= n < NT else None
                ffn(at, shared=i - 2 < TT)
                for turn in turns.get(i, []):
                    turn()
            pipeline(dve, TT + 2, TT + 4, NT - 1, NT + 2, NT, ffn)

        @block.tensor
        def _(pe):
            def products(out, terms, done):
                n = len(terms) * 3
                q = 0
                for (ah, al), (bh, bl) in terms:
                    for a, b in ((ah, bh), (ah, bl), (al, bh)):
                        last = pe.matmul(out, a, b, start=q == 0, stop=q == n - 1)
                        q += 1
                if done is not None:
                    last.then_inc(done, 1)

            def transposes(out, of, starts, done):
                for c, at_ in enumerate(starts):
                    last = pe.transpose(out[:, c * P:(c + 1) * P], of[:, at_:at_ + P], ident[:, :])
                last.then_inc(done, 1)

            def both(hi, lo, p, k):
                return hi[:, p, k * P:(k + 1) * P], lo[:, p, k * P:(k + 1) * P]

            def four(out, hi, lo, p, done):
                for b in range(2):
                    cols = slice(b * 2 * D, (b + 1) * 2 * D)
                    terms = [(both(hi, lo, p, k), (ctx_hi[:, k, cols], ctx_lo[:, k, cols])) for k in range(KD)]
                    products(out[:, b, :], terms, done if b else None)

            def layer1(i):
                a, b, c, d, e, f = i + 1, i, i - 1, i - 1, i - 3, i - 4
                if 0 <= c < TT:
                    pe.wait_ge(s_hid1, c + 1)
                    if c:
                        pe.wait_ge(s_hlo1, c)
                    transposes(ps_hid, hid[:, c % 2, :], range(0, D, P), s_C1)
                if 0 <= b < TT:
                    pe.wait_ge(s_lo1, b + 1)
                    if b == 0:
                        pe.wait_ge(s_ctxlo, KD)
                    else:
                        pe.wait_ge(s_pick, b)
                    four(ps_up[0], inT_hi, inT_lo, b % 2, s_B1)
                if 0 <= a < TT:
                    pe.wait_ge(s_n1, a + 1)
                    if a:
                        pe.wait_ge(s_lo1, a)
                    transposes(ps_in, normed[:, a % 2, :], range(0, D, P), s_A1)
                if 0 <= e < TT:
                    pe.wait_ge(s_h2, e + 1)
                    if e:
                        pe.wait_ge(s_h2T, e)
                    transposes(ps_y, h2[:, e % 2, :], range(0, D, P), s_E1)
                if 0 <= f < TT:
                    if f == 0:
                        pe.wait_ge(s_wr, 16)
                    else:
                        pe.wait_ge(s_lg, f)
                    pe.wait_ge(s_h2T, f + 1)
                    for k in range(KD):
                        last = pe.matmul(ps_r[:, 0:E], h2T[:, k * P:(k + 1) * P], wr_sb[:, k, :], start=k == 0,
                                         stop=k == KD - 1)
                    last.then_inc(s_F1, 1)
                if 0 <= d < TT:
                    pe.wait_ge(s_hlo1, d + 1)
                    if d:
                        pe.wait_ge(s_x2, d)
                    four(ps_y4, hidT_hi, hidT_lo, d % 2, s_D1)

            def rank():
                pe.wait_ge(s_taken, 1)
                pe.wait_ge(s_lg, TT)
                out = ps_r[:, 0:(TT + 1) * E].rearrange("p (t e) -> p t e", e=E)
                pe.matmul(out, below[:, :], taken[:, :, :], start=True, stop=False)
                for t in range(TT):
                    n = TT - t
                    last = pe.matmul(out[:, t + 1:, :], ones[:, :],
                                     taken[:, t, :].unsqueeze(1).to_broadcast([P, n, E]),
                                     start=False, stop=t == TT - 1)
                last.then_inc(s_rank, 1)

            def invert():
                C = TOPK * TT
                pe.wait_ge(s_vals, 1)
                for c in range(C):
                    pe.wait_ge(s_looh, c + 1)
                    pe.matmul(ps_r[:, 128:128 + 2 * RT], looh[:, c, :].bitcast(fp32),
                              vals[:, c, :, :].rearrange("p v r -> p (v r)"),
                              start=c == 0, stop=c == C - 1).then_inc(s_inv, 1)

            def expert(j):
                if isinstance(j.n, int) and j.n < TT:
                    return 0
                return pe.value_load(te[0:1, bass.ds(j.n - TT, 1)], min_val=1, max_val=E)

            def rows_ready(j):
                if isinstance(j.n, int) and j.n < TT:
                    pe.wait_ge(s_rows[j.p], 16 * (j.before + 1))
                else:
                    pe.wait_ge(s_gath[j.p], 16 * (j.before - TT // 2 + 1))

            experts = {}

            def ffn(at):
                if at(1):
                    experts[at(1).n] = expert(at(1))
                if j := at(1):
                    rows_ready(j)
                    if not (isinstance(j.n, int) and j.n == 0):
                        pe.wait_ge(s_lo, j.n)
                    transposes(ps_in, rows[:, j.p, :], range(0, D, P), s_A)
                if j := at(-1):
                    pe.wait_ge(s_hid, j.n + 1)
                    if not (isinstance(j.n, int) and j.n == 0):
                        pe.wait_ge(s_hlo, j.n)
                    transposes(ps_hid, hid[:, j.p, :], HC, s_C)
                if j := at(-2):
                    pe.wait_ge(s_hlo, j.n + 1)
                    if not (isinstance(j.n, int) and j.n == 0):
                        pe.wait_ge(s_y, j.n)
                    terms = [(both(hidT_hi, hidT_lo, j.p, c),
                              tuple(w[:, experts[j.n], c * D:(c + 1) * D] for w in (w2_hi, w2_lo))) for c in range(NHC)]
                    products(ps_y[:, 0:D], terms, s_D)
                if j := at(1):
                    pe.wait_ge(s_lo, j.n + 1)
                    if not (isinstance(j.n, int) and j.n < 2):
                        pe.wait_ge(s_hid, j.n - 1)
                    for half in range(2):
                        terms = [(both(inT_hi, inT_lo, j.p, k),
                                  tuple(w[:, experts[j.n], k * U1 + half * HP:k * U1 + (half + 1) * HP] for w in (w13_hi, w13_lo)))
                                 for k in range(KD)]
                        products(ps_up[j.p][:, half, 0:HP], terms, s_B if half else None)

            pe.wait_ge(s_eye, 1)
            for i in range(-1, TT + 2):
                layer1(i)
            pe.wait_ge(s_ulo, UNITS)
            pe.wait_ge(s_pick, TT)
            ffn(lambda k: Tile(0, 0, 0) if k == 1 else None)
            layer1(TT + 2)
            layer1(TT + 3)
            rank()
            for i in range(0, TT + 2):
                def at(k, i=i):
                    n = i + k
                    return Tile(n, n % 2, n // 2) if 0 <= n < NT else None
                if i == 0:
                    pe.wait_ge(s_x2, TT)
                if i == 4:
                    invert()
                if i == TT - 1:
                    pe.wait_ge(s_te, 1)
                    pe.wait_ge(s_ulo, (E + 1) * UNITS)
                ffn(at)
            pipeline(pe, TT + 2, TT + 2, TT + 2, NT + 2, NT, ffn)


def kernel(x, itok_BxS_13_99985, ctx_2048, L0_ffn_sw1, L0_ffn_sw2, L0_ffn_sw3, L0_ffn_ew1, L0_ffn_ew2, L0_ffn_ew3,
           L0_ffn_wr):
    import concourse.bacc as bacc
    import numpy as np
    from concourse.bass_utils import run_bass_kernel_spmd

    def arr(a):
        return np.ascontiguousarray(np.asarray(a))

    x, ctx = arr(x), arr(ctx_2048)
    ids = arr(itok_BxS_13_99985)
    w1 = np.concatenate([arr(L0_ffn_sw1)[None], arr(L0_ffn_ew1)])
    w3 = np.concatenate([arr(L0_ffn_sw3)[None], arr(L0_ffn_ew3)])
    w2 = np.concatenate([arr(L0_ffn_sw2)[None], arr(L0_ffn_ew2)])
    arrays = {
        "x": x.reshape(T, D),
        "ids": arr(ids.reshape(TT, P).T),
        "ctx": arr(ctx.transpose(2, 0, 1).reshape(D, CE * D)),
        "w13": arr(np.stack([w1, w3], 1).transpose(0, 3, 1, 2)),
        "w2": arr(w2.transpose(0, 2, 1)),
        "wr": arr(arr(L0_ffn_wr).T),
    }
    nc = bacc.Bacc("TRN2", target_bir_lowering=False, num_devices=1)
    aps = [nc.dram_tensor("in_" + n, a.shape, mybir.dt.from_np(a.dtype), kind="ExternalInput").ap() for n, a in arrays.items()]
    out = nc.dram_tensor("out", (T, D), fp32, kind="ExternalOutput").ap()
    build(nc, *aps, out)
    r = run_bass_kernel_spmd(nc, [{"in_" + n: a for n, a in arrays.items()}], core_ids=[0])
    return r.results[0]["out"].reshape(x.shape)
```

```python
from collections import namedtuple
from contextlib import ExitStack

import concourse.bass as bass
from concourse import mybir

P = 128
T = 1024
D = 256
KD = D // P
TT = T // P
CE = 4
VOCAB = 12500
VSTEP = VOCAB // CE
E = 8
TOPK = 2
H = D * 4 // 3
HP = H + H % 2
NHC = -(-H // P)
HC = [min(c * P, H - P) for c in range(NHC)]
LAST = H - (NHC - 1) * P
RT = (TOPK * T + E * (P - 1)) // P
NT = TT + RT
WARM = {-1: 32, 0: 16, 1: 26}
WARM_FFN = 20
NPL = 6
LATE = 2
NX = 3
EPS = 1e-5
U1 = 2 * HP
UNITS = KD + 1
UNIT_AT = [u * U1 for u in range(UNITS)] + [KD * U1 + NHC * D]

fp32 = mybir.dt.float32
f32r = mybir.dt.float32r
bf16 = mybir.dt.bfloat16
i32 = mybir.dt.int32
u32 = mybir.dt.uint32
ALU = mybir.AluOpType
ACT = mybir.ActivationFunctionType
AX = mybir.AxisListType.X

Tile = namedtuple("Tile", "n p before")


def tile(g, c):
    return Tile(g * 2 + c, c % 2, g + c // 2)


def build(nc, x_d, ids_d, ctx_d, w13_d, w2_d, wr_d, out_d):
    es = ExitStack()
    with es:
        def sb(name, shape, dt=fp32):
            return es.enter_context(nc.sbuf_tensor(name, shape, dt))

        def sem(name):
            return es.enter_context(nc.semaphore(name))

        x2_dram = nc.dram_tensor("x2_rows", (T, D), fp32).ap()
        h2T_dram = nc.dram_tensor("h2_transposed_rows", (T, D), fp32).ap()
        h2_dram = nc.dram_tensor("h2_rows", (T, D), fp32).ap()

        ctx_hi = sb("ctx_hi", [P, KD, CE * D], f32r)
        ctx_lo = sb("ctx_lo", [P, KD, CE * D], f32r)
        w13_hi = sb("w13_hi", [P, E + 1, KD * U1], f32r)
        w13_lo = sb("w13_lo", [P, E + 1, KD * U1], f32r)
        w2_hi = sb("w2_hi", [P, E + 1, NHC * D], f32r)
        w2_lo = sb("w2_lo", [P, E + 1, NHC * D], f32r)
        stage = sb("stage", [P, UNIT_AT[-1]])
        wr_sb = sb("wr_sb", [P, KD, E])

        rows = sb("rows", [P, 2, D])
        normed = sb("normed", [P, 2, D])
        inT_hi = sb("inT_hi", [P, 2, D], f32r)
        inT_lo = sb("inT_lo", [P, 2, D], f32r)
        picked = sb("picked", [P, D])
        silu = sb("silu", [P, HP])
        hid = sb("hid", [P, 2, HP])
        hidT_hi = sb("hidT_hi", [P, 2, NHC * P], f32r)
        hidT_lo = sb("hidT_lo", [P, 2, NHC * P], f32r)
        x2 = sb("x2", [P, NX, D])
        h2 = sb("h2", [P, 2, D])
        h2T = sb("h2T", [P, D])
        y_sb = normed
        stats = sb("stats", [P, 2, 6])
        mv = sb("mv", [P, 2, 2])
        rstd = sb("rstd", [P, 2, 2])
        stats2 = sb("stats2", [P, 2, 6])
        mv2 = sb("mv2", [P, 2, 2])
        minus_one = sb("minus_one", [P, 1])
        minus_half = sb("minus_half", [P, 2])
        var = sb("var", [P, 2, 2])
        warm = sb("warm", [P, 1])
        N_CONST = 9

        C = TOPK * TT
        ids = sb("ids", [P, TT], i32)
        idf = sb("idf", [P, TT])
        ge = sb("ge", [P, CE + 1, TT])
        mine = sb("mine", [P, TT, CE])
        iota = sb("iota", [P, P])
        part = sb("part", [P, 1])
        spare = sb("spare", [P, 1])
        nspare = sb("nspare", [P, 1])
        tile1 = sb("tile1", [P, TT])
        k128 = sb("k128", [P, E, TT])
        ident = sb("ident", [P, P])
        below = sb("below", [P, P], bf16)
        ones = sb("ones", [P, P], bf16)
        ones8 = sb("ones8", [P, E])
        lg = sb("lg", [P, TT, E])
        top8 = sb("top8", [P, TT, E])
        top8_at = sb("top8_at", [P, TT, E], u32)
        chosen = sb("chosen", [P, TOPK, TT])
        oh = sb("oh", [P, TOPK, TT, E])
        taken = sb("taken", [P, TT + 1, E], bf16)
        sm = sb("sm", [P, TT, E])
        ssum = sb("ssum", [P, TT])
        tp = sb("tp", [P, TOPK, TT])
        smk = picked[:, 0:C * E].rearrange("p (k t e) -> p k t e", k=TOPK, t=TT)
        fold = picked[:, C * E:C * E * 3 // 2].rearrange("p (k t e) -> p k t e", k=TOPK, t=TT)
        gate = sb("gate", [P, TOPK, TT])
        tpx = sb("tpx", [P, TOPK, TT, E])
        cmpk = sb("cmpk", [P, E, TT])
        ntl = sb("ntl", [P, E])
        fend = sb("fend", [P, E])
        base = sb("base", [P, E])
        slot_e = sb("slot_e", [P, TT, E])
        pos = sb("pos", [P, TOPK, TT])
        posi = sb("posi", [P, TOPK * TT], i32)
        loi = sb("loi", [P, TOPK * TT], i32)
        hii = sb("hii", [P, TOPK * TT], i32)
        lof = sb("lof", [P, TOPK * TT])
        hif = sb("hif", [P, TOPK * TT])
        gpart = sb("gpart", [P, 2, TOPK * TT], bf16)
        grest = sb("grest", [P, 2, TOPK * TT])
        tok = sb("tok", [P, RT])
        cmpj = sb("cmpj", [P, RT, E])
        tef = sb("tef", [P, RT])
        te = sb("te", [P, RT], i32)
        cuts, at_ = [], 0
        for n in (C * P, C * RT, C * 2 * RT, C * 3 * RT):
            cuts.append(stage[:, :].bitcast(bf16)[:, at_:at_ + n])
            at_ += n
        place1h = cuts[0].rearrange("p (c n) -> p c n", n=P)
        tile1h = cuts[1].rearrange("p (c r) -> p c r", c=C)
        tokens = cuts[2].rearrange("p (c v r) -> p c v r", c=C, v=2)
        gates3 = cuts[3].rearrange("p (c v r) -> p c v r", c=C, v=3)
        used = sb("used", [P, RT])
        off = sb("off", [P, RT])
        src = sb("src", [P, RT], u32)
        dst = sb("dst", [P, RT], u32)
        sgate = sb("sgate", [P, RT])

        ps = es.enter_context(nc.psum_tensor("ps", [P, 8, 512], fp32))
        ps_in = ps[:, 0, :]
        ps_up = [ps[:, 1:3, :], ps[:, 3:5, :]]
        ps_y4 = ps[:, 3:5, :]
        ps_hid = ps[:, 5, :]
        ps_y = ps[:, 6, :]
        ps_r = ps[:, 7, :]
        inv_tok = ps[:, 7, 128:128 + 2 * RT].rearrange("p (v r) -> p v r", v=2)
        inv_gate = ps[:, 7, 256:256 + 3 * RT].rearrange("p (v r) -> p v r", v=3)

        s_ctx = [sem(f"ctx_loaded{e}") for e in range(CE)]
        s_wr, s_ids = sem("wr_loaded"), sem("ids_loaded")
        s_ctxhi, s_ctxlo = sem("ctx_hi_done"), sem("ctx_lo_done")
        s_ones, s_iota = sem("ones_made"), sem("iota_made")
        s_const, s_eye = sem("constants"), sem("matrices_made")
        s_unit = [sem(f"unit_loaded{u}") for u in range(UNITS)]
        s_uhi, s_ulo = sem("unit_hi_done"), sem("unit_lo_done")
        s_mine = sem("mine")
        s_x = [sem("x_loaded0"), sem("x_loaded1")]
        s_xres = [sem(f"x_residual_loaded{b}") for b in range(NX)]
        s_var1, s_var2 = sem("var1"), sem("var2")
        s_pick0, s_pickp, s_x2p = sem("picked0"), sem("picked_part"), sem("x2_part")
        s_st1, s_mv1, s_rs, s_n1 = sem("stats1"), sem("mv1"), sem("rstd"), sem("normed1")
        s_A1, s_hi1, s_lo1 = sem("in_transposed1"), sem("inT_hi1"), sem("inT_lo1")
        s_B1, s_pick, s_silu1, s_hid1 = sem("up1"), sem("picked"), sem("silu1"), sem("hid1")
        s_C1, s_hhi1, s_hlo1 = sem("hid_transposed1"), sem("hidT_hi1"), sem("hidT_lo1")
        s_D1, s_x2 = sem("down1"), sem("x2_ready")
        s_st2, s_mv2, s_h2 = sem("stats2"), sem("mv2"), sem("h2_ready")
        s_E1, s_h2T, s_F1, s_lg = sem("h2_transposed"), sem("h2T_copied"), sem("logits"), sem("logits_copied")
        s_x2st = [sem(f"x2_stored{b}") for b in range(NX)]
        s_h2st = [sem("h2_stored0"), sem("h2_stored1")]

        s_h2Tst = sem("h2T_stored")
        s_rows = [sem("h2T_loaded0"), sem("h2T_loaded1")]
        s_res = [sem("residual_loaded0"), sem("residual_loaded1")]
        s_gath = [sem("rows_gathered0"), sem("rows_gathered1")]
        s_A, s_hi, s_lo = sem("routed_in_transposed"), sem("inT_hi_done"), sem("inT_lo_done")
        s_B, s_silu, s_hid = sem("up_done"), sem("silu_done"), sem("hid_done")
        s_C, s_hhi, s_hlo = sem("hid_transposed"), sem("hidT_hi_done"), sem("hidT_lo_done")
        s_D, s_y = sem("down_done"), sem("y_ready")
        s_init = [sem("sums_started0"), sem("sums_started1")]
        s_spare = sem("spare_rows_written")
        s_added = sem("sum_added")

        s_dv = sem("vector_routing_step")
        s_pl = sem("gpsimd_routing_step")
        s_taken, s_rank, s_te = sem("taken"), sem("ranked"), sem("tile_experts")
        s_max8, s_at8 = sem("top8"), sem("top8_at")
        s_sm, s_exp = sem("softmax_shifted"), sem("softmax_exp")
        s_lof, s_place1h_first = sem("places_known"), sem("place_onehots_first")
        s_place1h, s_tokens, s_gates3 = sem("place_onehots"), sem("tokens_laid_out"), sem("gates_laid_out")
        s_inv, s_invg = sem("slot_tokens_summed"), sem("slot_gates_summed")
        s_slots = sem("slots_ready")
        block = es.enter_context(nc.Block())

        def unit(u, part_, e):
            return part_[0][:, e, u * U1:(u + 1) * U1] if u < KD else part_[1][:, e, :]

        def peeled(i):
            def at(k):
                n = i + k
                return Tile(n, n % 2, n // 2) if 0 <= n < NT else None
            return at

        def shared(j):
            return isinstance(j.n, int) and j.n < TT

        def in_T(j):
            return rows[:, j.p, :] if shared(j) else ps_in[:, 0:D]

        def inputs_next(at):
            j = at(1)
            return j if j is not None and not (shared(j) and j.n > 2) else None

        def inputs_ahead(at):
            j = at(2)
            return j if j is not None and shared(j) and j.n > 2 else None

        def up_of(j):
            return ps_up[0] if isinstance(j.n, int) and j.n == 1 else ps_up[j.p]

        def h2T_of(t):
            return h2T[:, :] if t < TT - 1 else picked[:, :]

        def store_results(eng, t):
            eng.wait_ge(s_h2, t + 1)
            eng.dma_start(h2_dram[bass.ts(t, P), :], h2[:, t % 2, :]).then_inc(s_h2st[t % 2], 16)
            eng.dma_start(x2_dram[bass.ts(t, P), :], x2[:, t % NX, :]).then_inc(s_x2st[t % NX], 16)

        def pipeline(eng, first, lo, hi, end, count, step):
            def alone(i):
                step(lambda k: Tile(i + k, (i + k) % 2, (i + k) // 2) if 0 <= i + k < count else None)
            for i in range(first, lo):
                alone(i)
            if hi > lo:
                with eng.Fori(lo // 2, hi // 2) as g:
                    for c in (0, 1):
                        step(lambda k: tile(g, c + k))
            for i in range(hi, end):
                alone(i)

        HI, LO = (w13_hi, w2_hi), (w13_lo, w2_lo)

        @block.sync
        def _(sp):
            def load_unit(e, u):
                if e > 0:
                    sp.wait_ge(s_ulo, (e - 1) * UNITS + u + 1)
                to = stage[:, UNIT_AT[u]:UNIT_AT[u + 1]]
                if u < KD:
                    sp.dma_start(to, w13_d[e, u * P:(u + 1) * P, :]).then_inc(s_unit[u], 16)
                else:
                    sp.dma_start(to.rearrange("p (c d) -> p c d", c=NHC),
                                 w2_d[e, :, :].rearrange("(c p) d -> p c d", p=P)).then_inc(s_unit[u], 16)

            def load_expert(e):
                for u in range(UNITS):
                    load_unit(e, u)

            def store_h2T(t):
                sp.wait_ge(s_h2T, t + 1)
                sp.dma_start(h2T_dram[bass.ts(t, P), :], h2T_of(t)).then_inc(s_h2Tst, 16)

            def load_rows(j):
                sp.dma_start(rows[:, j.p, :], h2T_dram[bass.ts(j.n, P), :]).then_inc(s_rows[j.p], 16)

            raw = stage[:, 0:KD * CE * D].rearrange("p (k n) -> p k n", k=KD)
            sp.dma_start(rows[:, 0, :], x_d[0:P, :]).then_inc(s_x[0], 16)
            for e in range(CE):
                cols = slice(e * D, (e + 1) * D)
                sp.dma_start(raw[:, :, cols], ctx_d.rearrange("(k p) n -> p k n", p=P)[:, :, cols]).then_inc(s_ctx[e], 16)
            sp.dma_start(rows[:, 1, :], x_d[P:2 * P, :]).then_inc(s_x[1], 16)
            for n in range(NX):
                sp.dma_start(x2[:, n, :], x_d[bass.ts(n, P), :]).then_inc(s_xres[n], 16)
            sp.dma_start(wr_sb[:, :, :], wr_d.rearrange("(k p) e -> p k e", p=P)).then_inc(s_wr, 16)
            sp.dma_start(out_d[T:T + P, :], x_d[0:P, :]).then_inc(s_spare, 16)
            sp.wait_ge(s_ctxlo, CE)
            for e in range(E - 1):
                load_expert(e)
                if e >= 3:
                    store_h2T(e - 3)
            sp.wait_ge(s_n1, TT)
            for p in (0, 1):
                sp.wait_ge(s_h2Tst, 16 * (p + 1))
                load_rows(Tile(p, p, 0))
            load_expert(E - 1)
            store_h2T(E - 4)
            for n in (2, 3):
                sp.wait_ge(s_h2Tst, 16 * (n + 1))
                sp.wait_ge(s_lo, n - 1)
                load_rows(Tile(n, n % 2, n // 2))
            load_unit(E, 0)
            store_results(sp, TT - LATE)
            store_h2T(E - 3)
            for u in range(1, UNITS):
                load_unit(E, u)

            def load_residual(j):
                sp.dma_start(x2[:, j.p, :], x2_dram[bass.ts(j.n, P), :]).then_inc(s_res[j.p], 16)

            def shared_rows(at):
                if at(3):
                    sp.wait_ge(s_lo, at(2).n)
                    load_rows(at(3))
                if j := at(-2):
                    sp.wait_ge(s_y, j.n + 1)
                    sp.dma_start(out_d[bass.ts(j.n, P), :], y_sb[:, j.p, :]).then_inc(s_init[j.p], 16)
                    if at(0):
                        load_residual(at(0))

            store_h2T(TT - 2)
            store_h2T(TT - 1)
            store_results(sp, TT - 1)
            sp.wait_ge(s_lo, 3)
            load_rows(Tile(4, 0, 2))
            for p in (0, 1):
                sp.wait_ge(s_h2st[p], 16 * (TT // 2))
            sp.wait_ge(s_h2Tst, 16 * TT)
            for b in range(NX):
                sp.wait_ge(s_x2st[b], 16 * len(range(b, TT, NX)))
            for p in (0, 1):
                load_residual(Tile(p, p, 0))
            pipeline(sp, 2, 2, TT - 4, TT + 2, TT, shared_rows)
            sp.wait_ge(s_added, 16 * RT)

        @block.gpsimd
        def _(pool):
            pool.memset(ones[:, :], 1.0).then_inc(s_ones, 1)
            one = dict(allow_small_or_imprecise_dtypes=True)
            pool.iota(iota[:, :], [[1, P]], base=0, channel_multiplier=0, **one).then_inc(s_iota, 1)
            pool.iota(part[:, :], [[1, 1]], base=0, channel_multiplier=1, **one).then_inc(s_iota, 1)
            pool.memset(minus_half[:, :], -0.5).then_inc(s_const, 1)
            pool.memset(ones8[:, :], 1.0).then_inc(s_const, 1)
            pool.memset(minus_one[:, :], -1.0).then_inc(s_const, 1)
            pool.memset(taken[:, TT, :], 0.0).then_inc(s_const, 1)
            pool.iota(spare[:, :], [[1, 1]], base=T + P, channel_multiplier=1, **one).then_inc(s_const, 1)
            pool.iota(nspare[:, :], [[1, 1]], base=-(T + P), channel_multiplier=-1, **one).then_inc(s_const, 1)
            pool.iota(tile1[:, :], [[1, TT]], base=1, channel_multiplier=0, **one).then_inc(s_const, 1)
            pool.iota(k128[:, :, :], [[0, E], [P, TT]], base=0, channel_multiplier=0, **one).then_inc(s_const, 1)
            pool.memset(base[:, 0:1], 0.0).then_inc(s_const, 1)

            def low(n):
                e, u = divmod(n, UNITS)
                pool.wait_ge(s_uhi, n + 1)
                pool.tensor_tensor(unit(u, LO, e), stage[:, UNIT_AT[u]:UNIT_AT[u + 1]],
                                   unit(u, HI, e).bitcast(fp32), ALU.subtract).then_inc(s_ulo, 1)

            first = [0] + [UNITS] * (E - 1) + [UNITS - 1]
            first = [sum(first[:i + 1]) for i in range(E + 1)] + [(E + 1) * UNITS - 3, (E + 1) * UNITS]
            pool.wait_ge(s_const, 1)
            for i in range(-2, TT + 2):
                cols = [c for c, n in ((0, i - 2), (1, i + 2)) if 0 <= n < TT]
                if 0 in cols:
                    pool.wait_ge(s_var2, i - 1)
                if 1 in cols:
                    pool.wait_ge(s_var1, i + 3)
                cut = slice(cols[0], cols[-1] + 1)
                pool.tensor_tensor(rstd[:, i % 2, cut], var[:, i % 2, cut], minus_half[:, 0:len(cols)],
                                   ALU.pow).then_inc(s_rs, 1)
                if i >= 0:
                    for n in range(first[i], first[i + 1]):
                        low(n)

            steps = [0]

            def link(ins):
                steps[0] += 1
                ins.then_inc(s_pl, 1)
                pool.wait_ge(s_pl, steps[0])

            def sum_experts(out, of, halves):
                n = E // 2
                link(pool.tensor_tensor(halves[..., 0:n], of[..., 0:n], of[..., n:2 * n], ALU.add))
                while n > 2:
                    n //= 2
                    link(pool.tensor_tensor(halves[..., 0:n], halves[..., 0:n], halves[..., n:2 * n], ALU.add))
                link(pool.tensor_tensor(out, halves[..., 0], halves[..., 1], ALU.add))

            pool.wait_ge(s_const, N_CONST)
            pool.wait_ge(s_exp, 1)
            pool.wait_ge(s_h2Tst, 16 * TT)
            sum_experts(ssum[:, :], sm[:, :, :], fold[:, 0, :, :])
            link(pool.tensor_tensor(ssum[:, :], ssum[:, :], minus_one[:, :].to_broadcast([P, TT]), ALU.pow))
            pool.wait_ge(s_lof, 1)
            for c in range(NPL):
                pool.tensor_scalar(place1h[:, c, :], iota[:, :], lof[:, c:c + 1], None,
                                   ALU.is_equal).then_inc(s_place1h_first, 1)
            link(pool.tensor_tensor(sm[:, :, :], sm[:, :, :], ssum[:, :].unsqueeze(2).to_broadcast([P, TT, E]),
                                    ALU.mult))
            for k in range(TOPK):
                last = pool.tensor_tensor(smk[:, k, :, :], sm[:, :, :], oh[:, k, :, :], ALU.mult)
            link(last)
            sum_experts(tp[:, :, :], smk[:, :, :, :], fold[:, :, :, :])
            link(pool.tensor_tensor(ssum[:, :], tp[:, 0, :], tp[:, 1, :], ALU.add))
            link(pool.tensor_tensor(ssum[:, :], ssum[:, :], minus_one[:, :].to_broadcast([P, TT]), ALU.pow))
            link(pool.tensor_tensor(gate[:, :, :], tp[:, :, :], ssum[:, :].unsqueeze(1).to_broadcast([P, TOPK, TT]),
                                    ALU.mult))
            g = gate[:, :, :].rearrange("p k t -> p (k t)")
            link(pool.tensor_copy(gpart[:, 0, :], g))
            link(pool.tensor_tensor(grest[:, 0, :], g, gpart[:, 0, :], ALU.subtract))
            link(pool.tensor_copy(gpart[:, 1, :], grest[:, 0, :]))
            link(pool.tensor_tensor(grest[:, 1, :], grest[:, 0, :], gpart[:, 1, :], ALU.subtract))

            def gate_lists():
                pool.wait_ge(s_tokens, 1)
                for v, of in enumerate((gpart[:, 0, :], gpart[:, 1, :], grest[:, 1, :])):
                    pool.tensor_tensor(gates3[:, :, v, :], tile1h, of.unsqueeze(2).to_broadcast([P, C, RT]),
                                       ALU.mult).then_inc(s_gates3, 1)

            pool.wait_ge(s_slots, 2)
            for r in range(-2, RT + 3):
                if r == 0:
                    gate_lists()
                if r + 2 < RT:
                    n = r + 2
                    if n < 2:
                        pool.wait_ge(s_lo, n + TT - 1)
                    else:
                        pool.wait_ge(s_A, n - 1)
                    pool.indirect_dma_start(out=rows[:, n % 2, :], out_offset=None, in_=h2_dram,
                                            in_offset=bass.IndirectOffsetOnAxis(ap=src[:, n:n + 1], axis=0),
                                            ).then_inc(s_gath[n % 2], 16)
                if r - 3 >= 0:
                    n = r - 3
                    pool.wait_ge(s_y, n + TT + 1)
                    if n == 0:
                        pool.wait_ge(s_spare, 16)
                        for p in (0, 1):
                            pool.wait_ge(s_init[p], 16 * (TT // 2))
                    else:
                        pool.wait_ge(s_added, n * 16)
                    pool.indirect_dma_start(out=out_d, in_=y_sb[:, n % 2, :], in_offset=None,
                                            out_offset=bass.IndirectOffsetOnAxis(ap=dst[:, n:n + 1], axis=0),
                                            compute_op=ALU.add).then_inc(s_added, 16)

        @block.scalar
        def _(act):
            def load_x(t):
                act.dma_start(rows[:, t % 2, :], x_d[bass.ts(t, P), :]).then_inc(s_x[t % 2], 16)

            def high(n):
                e, u = divmod(n, UNITS)
                act.wait_ge(s_unit[u], 16 * (e + 1))
                act.activation(unit(u, HI, e), stage[:, UNIT_AT[u]:UNIT_AT[u + 1]], ACT.Copy).then_inc(s_uhi, 1)

            act.dma_start(ids[:, :], ids_d).then_inc(s_ids, 16)
            act.wait_ge(s_iota, 2)
            act.activation(warm[:, :], part[:, :], ACT.Silu)
            raw = stage[:, 0:KD * CE * D].rearrange("p (k n) -> p k n", k=KD)

            def ctx_high(e):
                cols = slice(e * D, (e + 1) * D)
                act.wait_ge(s_ctx[e], 16)
                act.activation(ctx_hi[:, :, cols], raw[:, :, cols], ACT.Copy).then_inc(s_ctxhi, 1)

            for e in range(CE // 2):
                ctx_high(e)

            def silu_of(j):
                act.wait_ge(s_B, j.n + 1)
                if not (isinstance(j.n, int) and j.n == 0):
                    act.wait_ge(s_hid, j.n)
                act.activation(silu[:, :], up_of(j)[:, 0, 0:HP], ACT.Silu).then_inc(s_silu, 1)

            def input_high(j):
                if j is not None:
                    if shared(j):
                        act.wait_ge(s_rows[j.p], 16 * (j.before + 1))
                    else:
                        act.wait_ge(s_A, j.n - TT + 1)
                    act.activation(inT_hi[:, j.p, :], in_T(j), ACT.Copy).then_inc(s_hi, 1)

            def hidden_high(at):
                if j := at(-1):
                    act.wait_ge(s_C, j.n + 1)
                    act.activation(hidT_hi[:, j.p, :], ps_hid[:, 0:NHC * P], ACT.Copy).then_inc(s_hhi, 1)

            def ffn(at):
                if j := at(0):
                    silu_of(j)
                input_high(inputs_next(at))
                hidden_high(at)
                input_high(inputs_ahead(at))

            def silu_last(at):
                hidden_high(at)
                silu_of(at(0))
                input_high(inputs_ahead(at))

            for i in range(-1, TT + 3):
                a, b, c, e = i + 1, i, i - 1, i - 3
                if 0 <= c < TT:
                    act.wait_ge(s_C1, c + 1)
                    act.activation(hidT_hi[:, c % 2, 0:D], ps_hid[:, 0:D], ACT.Copy).then_inc(s_hhi1, 1)
                if i == TT:
                    ffn(peeled(0))
                if 0 <= e < TT - LATE:
                    store_results(act, e)
                if 0 <= i - 1 < E:
                    high(i * UNITS - 1)
                if 0 <= b < TT:
                    act.wait_ge(s_B1, b + 1)
                    if b:
                        act.wait_ge(s_hid1, b)
                    act.activation(picked[:, :], ps_up[0][:, 0, 0:D], ACT.Copy,
                                   scale=mine[:, b, 0:1]).then_inc(s_pick0, 1)
                if 0 <= a < TT:
                    act.wait_ge(s_A1, a + 1)
                    act.activation(inT_hi[:, a % 2, :], ps_in[:, 0:D], ACT.Copy).then_inc(s_hi1, 1)
                    if a == 0:
                        for e_ in range(CE // 2, CE):
                            ctx_high(e_)
                    if a + 2 < TT:
                        load_x(a + 2)
                if a == TT:
                    ffn(peeled(-1))
                if i == TT + 1:
                    silu_of(peeled(1)(0))
                    hidden_high(peeled(1))
                    input_high(inputs_next(peeled(1)))
                if 0 <= e < TT:
                    act.wait_ge(s_E1, e + 1)
                    if 0 < e < TT - 1:
                        act.wait_ge(s_F1, e)
                        act.wait_ge(s_h2Tst, 16 * e)
                    act.activation(h2T_of(e), ps_y[:, 0:D], ACT.Copy).then_inc(s_h2T, 1)
                if i > TT:
                    high(E * UNITS + i - TT)
                if i == TT + 2:
                    act.activation(warm[:, :], minus_one[:, :], ACT.Exp)
                    input_high(inputs_ahead(peeled(1)))
                if 0 <= i <= E:
                    high(i * UNITS)
                if 0 <= b < TT:
                    act.wait_ge(s_pick, b + 1)
                    act.activation(silu[:, 0:D], picked[:, :], ACT.Silu).then_inc(s_silu1, 1)
                if 0 <= i < E:
                    for u in range(1, UNITS - 1):
                        high(i * UNITS + u)
                if NX <= i < TT:
                    act.wait_ge(s_x2st[i % NX], 16 * (i // NX))
                    act.dma_start(x2[:, i % NX, :], x_d[bass.ts(i, P), :]).then_inc(s_xres[i % NX], 16)
            act.wait_ge(s_sm, 1)
            act.activation(sm[:, :, :], sm[:, :, :], ACT.Exp).then_inc(s_exp, 1)
            silu_last(peeled(2))
            pipeline(act, 3, TT, NT - 1, NT + 1, NT, ffn)

        @block.vector
        def _(dve):
            steps = [0]

            def link(ins):
                steps[0] += 1
                ins.then_inc(s_dv, 1)
                dve.wait_ge(s_dv, steps[0])

            def stats1(n):
                p = n % 2
                dve.wait_ge(s_x[p], 16 * (n // 2 + 1))
                dve.bn_stats(stats[:, p, :], rows[:, p, :]).then_inc(s_st1, 1)
                yield
                dve.wait_ge(s_st1, n + 1)
                dve.bn_aggr(mv[:, p, :], stats[:, p, :]).then_inc(s_mv1, 1)
                yield
                dve.wait_ge(s_mv1, n + 1)
                dve.tensor_scalar(var[:, p, 1:2], mv[:, p, 1:2], EPS, None, ALU.add).then_inc(s_var1, 1)
                yield

            def stats_h2(n):
                p = n % 2
                dve.wait_ge(s_x2, n + 1)
                dve.bn_stats(stats2[:, p, :], x2[:, n % NX, :]).then_inc(s_st2, 1)
                yield
                dve.wait_ge(s_st2, n + 1)
                dve.bn_aggr(mv2[:, p, :], stats2[:, p, :]).then_inc(s_mv2, 1)
                yield
                dve.wait_ge(s_mv2, n + 1)
                dve.tensor_scalar(var[:, p, 0:1], mv2[:, p, 1:2], EPS, None, ALU.add).then_inc(s_var2, 1)
                yield

            def norm1(n):
                p = n % 2
                if n >= 2:
                    dve.wait_ge(s_A1, n - 1)
                dve.wait_ge(s_rs, n + 1)
                dve.tensor_scalar(normed[:, p, :], rows[:, p, :], mv[:, p, 0:1], rstd[:, p, 1:2], ALU.subtract,
                                  ALU.mult).then_inc(s_n1, 1)

            def norm_h2(n):
                p = n % 2
                if n >= 2:
                    dve.wait_ge(s_h2st[p], 16 * (n // 2))
                dve.wait_ge(s_rs, n + 5)
                dve.tensor_scalar(h2[:, p, :], x2[:, n % NX, :], mv2[:, p, 0:1], rstd[:, p, 0:1], ALU.subtract,
                                  ALU.mult).then_inc(s_h2, 1)

            def in_turn(*steps_):
                chains = [iter(x) for x in steps_]
                while chains:
                    for x in list(chains):
                        if next(x, "end") == "end":
                            chains.remove(x)

            dve.wait_ge(s_iota, 2)
            link(dve.tensor_scalar(ident[:, :], iota[:, :], part[:, 0:1], None, ALU.is_equal))
            dve.tensor_scalar(below[:, :], iota[:, :], part[:, 0:1], None, ALU.is_gt).then_inc(s_eye, 1)
            in_turn(stats1(0))
            dve.wait_ge(s_ids, 16)
            link(dve.tensor_copy(idf[:, :], ids[:, :]))
            for e in range(1, CE):
                last = dve.tensor_scalar(ge[:, e, :], idf[:, :], float(e * VSTEP), None, ALU.is_ge)
            link(last)
            mt = mine[:, :, :].rearrange("p t e -> p e t")
            dve.tensor_scalar(mt[:, 0, :], ge[:, 1, :], -1.0, 1.0, ALU.mult, ALU.add)
            dve.tensor_tensor(mt[:, 1:CE - 1, :], ge[:, 1:CE - 1, :], ge[:, 2:CE, :], ALU.subtract)
            dve.tensor_copy(mt[:, CE - 1, :], ge[:, CE - 1, :]).then_inc(s_mine, 1)
            norm1(0)

            def ctx_low(e):
                cols = slice(e * D, (e + 1) * D)
                dve.wait_ge(s_ctxhi, e + 1)
                dve.tensor_tensor(ctx_lo[:, :, cols], raw[:, :, cols], ctx_hi[:, :, cols].bitcast(fp32),
                                  ALU.subtract).then_inc(s_ctxlo, 1)

            raw = stage[:, 0:KD * CE * D].rearrange("p (k n) -> p k n", k=KD)
            for e in range(CE // 2):
                ctx_low(e)
            dve.wait_ge(s_mine, 1)

            def pick(out, src4, n, start, done_part, done):
                for e in range(start, CE):
                    at_ = src4[:, e // 2, (e % 2) * D:(e % 2 + 1) * D]
                    dve.scalar_tensor_tensor(out, at_, mine[:, n, e:e + 1], out, ALU.mult, ALU.add)\
                       .then_inc(done if e == CE - 1 else done_part, 1)
                    yield
                    if e < CE - 1:
                        dve.wait_ge(done_part, n * (CE - 1 - start) + e - start + 1)

            def down(n):
                dve.wait_ge(s_D1, n + 1)
                dve.wait_ge(s_xres[n % NX], 16 * (n // NX + 1))
                return pick(x2[:, n % NX, :], ps_y4, n, 0, s_x2p, s_x2)

            def input_low(j):
                if j is not None:
                    dve.wait_ge(s_hi, j.n + 1)
                    dve.tensor_tensor(inT_lo[:, j.p, :], in_T(j), inT_hi[:, j.p, :].bitcast(fp32),
                                      ALU.subtract).then_inc(s_lo, 1)

            def ffn(at, before_hidT=None, before_hid=None, alone=False):
                if not alone:
                    input_low(inputs_next(at))
                if before_hidT is not None:
                    before_hidT()
                if j := at(-1):
                    dve.wait_ge(s_hhi, j.n + 1)
                    dve.tensor_tensor(hidT_lo[:, j.p, :], ps_hid[:, 0:NHC * P], hidT_hi[:, j.p, :].bitcast(fp32),
                                      ALU.subtract).then_inc(s_hlo, 1)
                if before_hid is not None:
                    before_hid()
                if j := at(0):
                    dve.wait_ge(s_silu, j.n + 1)
                    dve.tensor_tensor(hid[:, j.p, 0:HP], silu[:, :], up_of(j)[:, 1, 0:HP], ALU.mult).then_inc(s_hid, 1)
                if not alone:
                    input_low(inputs_ahead(at))
                if j := at(-2):
                    dve.wait_ge(s_D, j.n + 1)
                    if shared(j):
                        dve.wait_ge(s_res[j.p], 16 * (j.before + 1))
                        if j.n >= 2:
                            dve.wait_ge(s_init[j.p], 16 * j.before)
                        dve.tensor_tensor(y_sb[:, j.p, :], ps_y[:, 0:D], x2[:, j.p, :], ALU.add).then_inc(s_y, 1)
                    else:
                        r = j.n - TT
                        if isinstance(r, int) and r < 2:
                            dve.wait_ge(s_init[j.p], 16 * (TT // 2))
                        else:
                            dve.wait_ge(s_added, 16 * (r - 1))
                        dve.tensor_scalar(y_sb[:, j.p, :], ps_y[:, 0:D], sgate[:, bass.ds(r, 1)], None,
                                          ALU.mult).then_inc(s_y, 1)

            def copy_logits(n):
                dve.wait_ge(s_F1, n + 1)
                dve.tensor_copy(lg[:, n, :], ps_r[:, 0:E]).then_inc(s_lg, 1)

            def order_logits(n):
                dve.wait_ge(s_lg, n + 1)
                dve.max(top8[:, n, :], lg[:, n, :]).then_inc(s_max8, 1)

            def find_logits(n):
                dve.wait_ge(s_max8, n + 1)
                dve.max_index(top8_at[:, n, :], top8[:, n, :], lg[:, n, :]).then_inc(s_at8, 1)

            for i in range(-1, TT + 5):
                a, b, c, d, n = i + 1, i, i - 1, i - 2, i + 2
                if 0 <= i - 6 < TT:
                    find_logits(i - 6)
                if 0 <= i - 5 < TT:
                    order_logits(i - 5)

                def hidden_low():
                    dve.wait_ge(s_hhi1, c + 1)
                    dve.tensor_tensor(hidT_lo[:, c % 2, 0:D], ps_hid[:, 0:D], hidT_hi[:, c % 2, 0:D].bitcast(fp32),
                                      ALU.subtract).then_inc(s_hlo1, 1)

                if 0 <= c < TT - 1:
                    hidden_low()
                in_turn(down(d) if 0 <= d < TT else (), stats1(n) if 2 <= n < TT and i >= 0 else ())
                if c == TT - 1:
                    hidden_low()
                if i == TT:
                    ffn(peeled(0))
                if 0 <= b < TT:
                    dve.wait_ge(s_pick0, b + 1)
                in_turn(pick(picked[:, :], ps_up[0], b, 1, s_pickp, s_pick) if 0 <= b < TT else (),
                        stats_h2(d) if 0 <= d < TT else ())
                if 0 <= a < TT:
                    dve.wait_ge(s_hi1, a + 1)
                    dve.tensor_tensor(inT_lo[:, a % 2, :], ps_in[:, 0:D], inT_hi[:, a % 2, :].bitcast(fp32),
                                      ALU.subtract).then_inc(s_lo1, 1)
                if a == TT:
                    ffn(peeled(-1))
                if i == TT + 1:
                    copy_logits(i - 4)
                    ffn(peeled(1), before_hid=lambda: norm_h2(TT - 1), alone=True)
                    input_low(inputs_next(peeled(1)))
                if i == -1:
                    for e in range(CE // 2, CE):
                        ctx_low(e)
                    in_turn(stats1(1))
                if 0 <= b < TT:
                    dve.wait_ge(s_silu1, b + 1)
                    dve.tensor_tensor(hid[:, b % 2, 0:D], silu[:, 0:D], picked[:, :], ALU.mult).then_inc(s_hid1, 1)
                if 0 <= d < TT - 1:
                    norm_h2(d)
                if 0 <= n < TT:
                    norm1(n)
                if 0 <= i - 4 < TT and i != TT + 1:
                    copy_logits(i - 4)
            def over_t(x):
                return x.unsqueeze(1).to_broadcast([P, TT, E])

            def choose():
                dve.wait_ge(s_const, N_CONST)
                dve.wait_ge(s_at8, TT)
                link(dve.tensor_copy(chosen[:, :, :], top8_at[:, :, 0:TOPK].rearrange("p t k -> p k t")))
                link(dve.tensor_tensor(oh[:, :, :, :].rearrange("p k t e -> p (k t) e"),
                                       chosen[:, :, :].rearrange("p k t -> p (k t)").unsqueeze(2).to_broadcast([P, C, E]),
                                       iota[:, 0:E].unsqueeze(1).to_broadcast([P, C, E]), ALU.is_equal))
                dve.tensor_tensor(taken[:, 0:TT, :], oh[:, 0, :, :], oh[:, 1, :, :], ALU.add).then_inc(s_taken, 1)
                dve.tensor_tensor(sm[:, :, :], lg[:, :, :], top8[:, :, 0:1].to_broadcast([P, TT, E]),
                                  ALU.subtract).then_inc(s_sm, 1)

            def bases():
                dve.wait_ge(s_rank, 1)
                count = ps_r[:, TT * E:(TT + 1) * E]
                link(dve.tensor_tensor(cmpk[:, :, :], count.unsqueeze(2).to_broadcast([P, E, TT]), k128[:, :, :],
                                       ALU.is_gt))
                link(dve.tensor_reduce(ntl[:, :], cmpk[:, :, :], AX, ALU.add))
                link(dve.tensor_tensor_scan(base[:, 1:E], ones8[:, 1:E], ntl[:, 0:E - 1], 0.0, ALU.mult, ALU.add))

            def find_slots():
                rank = ps_r[:, 0:TT * E].rearrange("p (t e) -> p t e", t=TT)
                link(dve.scalar_tensor_tensor(slot_e[:, :, :], over_t(base[:, :]), float(P), rank, ALU.mult, ALU.add))
                link(dve.tensor_tensor(tpx[:, :, :, :], oh[:, :, :, :],
                                       slot_e[:, :, :].unsqueeze(1).to_broadcast([P, TOPK, TT, E]), ALU.mult))
                link(dve.tensor_reduce(pos[:, :, :], tpx[:, :, :, :], AX, ALU.add))

            def places():
                link(dve.tensor_copy(posi[:, :], pos[:, :, :].rearrange("p k t -> p (k t)")))
                dve.tensor_scalar(loi[:, :], posi[:, :], P - 1, None, ALU.bitwise_and)
                link(dve.tensor_scalar(hii[:, :], posi[:, :], P.bit_length() - 1, None, ALU.logical_shift_right))
                dve.tensor_copy(lof[:, :], loi[:, :]).then_inc(s_lof, 1)
                dve.wait_ge(s_lof, 1)
                link(dve.tensor_copy(hif[:, :], hii[:, :]))

            def place_onehots():
                n = C - NPL
                dve.tensor_tensor(place1h[:, NPL:, :], lof[:, NPL:].unsqueeze(2).to_broadcast([P, n, P]),
                                  iota[:, :].unsqueeze(1).to_broadcast([P, n, P]), ALU.is_equal).then_inc(s_place1h, 1)

            def token_lists():
                dve.wait_ge(s_ulo, (E + 1) * UNITS)
                link(dve.tensor_tensor(tile1h, hif[:, :].unsqueeze(2).to_broadcast([P, C, RT]),
                                       iota[:, 0:RT].unsqueeze(1).to_broadcast([P, C, RT]), ALU.is_equal))
                for k in range(TOPK):
                    dve.tensor_tensor(tokens[:, k * TT:(k + 1) * TT, 0, :], tile1h[:, k * TT:(k + 1) * TT, :],
                                      tile1[:, :].unsqueeze(2).to_broadcast([P, TT, RT]), ALU.mult)
                dve.tensor_scalar(tokens[:, :, 1, :], tile1h, part[:, 0:1], None, ALU.mult).then_inc(s_tokens, 1)

            def slots():
                dve.wait_ge(s_inv, 1)
                tile_of, place_of = inv_tok[:, 0, :], inv_tok[:, 1, :]
                dve.tensor_scalar(used[:, :], tile_of, 1.0, None, ALU.min)
                link(dve.tensor_scalar(tok[:, :], place_of, -float(P), None, ALU.add))
                link(dve.scalar_tensor_tensor(tok[:, :], tile_of, float(P), tok[:, :], ALU.mult, ALU.add))
                dve.tensor_scalar(src[:, :], tok[:, :], 0.0, None, ALU.max).then_inc(s_slots, 1)
                link(dve.tensor_scalar(off[:, :], used[:, :], nspare[:, 0:1], spare[:, 0:1], ALU.mult, ALU.add))
                dve.tensor_tensor(dst[:, :], tok[:, :], off[:, :], ALU.add).then_inc(s_slots, 1)

            def tile_experts():
                link(dve.tensor_tensor(fend[:, :], base[:, :], ntl[:, :], ALU.add))
                link(dve.tensor_tensor(cmpj[:, :, :], fend[:, :].unsqueeze(1).to_broadcast([P, RT, E]),
                                        iota[:, 0:RT].unsqueeze(2).to_broadcast([P, RT, E]), ALU.is_le))
                link(dve.tensor_reduce(tef[:, :], cmpj[:, :, :], AX, ALU.add))
                dve.tensor_scalar(te[:, :], tef[:, :], float(E - 1), 1.0, ALU.min, ALU.add).then_inc(s_te, 1)

            def slot_gates():
                dve.wait_ge(s_invg, 1)
                link(dve.tensor_copy(sgate[:, :], inv_gate[:, 2, :]))
                link(dve.tensor_tensor(sgate[:, :], sgate[:, :], inv_gate[:, 1, :], ALU.add))
                link(dve.tensor_tensor(sgate[:, :], sgate[:, :], inv_gate[:, 0, :], ALU.add))

            find_logits(TT - 1)
            choose()
            input_low(inputs_ahead(peeled(1)))
            turns = {2: [places], 3: [token_lists, place_onehots], 4: [slots], 5: [tile_experts], 9: [slot_gates]}
            for i in range(2, TT + 2):
                if i == 2:
                    ffn(peeled(i), before_hidT=bases, before_hid=find_slots)
                else:
                    ffn(peeled(i))
                for turn in turns.get(i, []):
                    turn()
            pipeline(dve, TT + 2, TT + 4, NT - 1, NT + 2, NT, ffn)

        @block.tensor
        def _(pe):
            def products(out, terms, done):
                n = len(terms) * 3
                q = 0
                for (ah, al), (bh, bl) in terms:
                    for a, b in ((ah, bh), (ah, bl), (al, bh)):
                        last = pe.matmul(out, a, b, start=q == 0, stop=q == n - 1)
                        q += 1
                if done is not None:
                    last.then_inc(done, 1)

            def transposes(out, of, starts, done):
                for c, at_ in enumerate(starts):
                    last = pe.transpose(out[:, c * P:(c + 1) * P], of[:, at_:at_ + P], ident[:, :])
                last.then_inc(done, 1)

            def both(hi, lo, p, k):
                return hi[:, p, k * P:(k + 1) * P], lo[:, p, k * P:(k + 1) * P]

            def four(out, hi, lo, p, done, first=False):
                for b in range(2):
                    if first:
                        pe.wait_ge(s_ctxlo, (b + 1) * CE // 2)
                    cols = slice(b * 2 * D, (b + 1) * 2 * D)
                    terms = [(both(hi, lo, p, k), (ctx_hi[:, k, cols], ctx_lo[:, k, cols])) for k in range(KD)]
                    products(out[:, b, :], terms, done if b else None)

            def layer1(i):
                a, b, c, d, e, f = i + 1, i, i - 1, i - 1, i - 3, i - 4
                if i == TT:
                    pe.wait_ge(s_ulo, UNITS)
                    pe.wait_ge(s_pick, TT)
                    experts[0] = 0
                    up(Tile(0, 0, 0))
                if 0 <= c < TT:
                    pe.wait_ge(s_hid1, c + 1)
                    if c:
                        pe.wait_ge(s_hlo1, c)
                    transposes(ps_hid, hid[:, c % 2, :], range(0, D, P), s_C1)
                if 0 <= b < TT:
                    pe.wait_ge(s_lo1, b + 1)
                    if b:
                        pe.wait_ge(s_pick, b)
                    four(ps_up[0], inT_hi, inT_lo, b % 2, s_B1, first=b == 0)
                if 0 <= a < TT:
                    pe.wait_ge(s_n1, a + 1)
                    if a:
                        pe.wait_ge(s_lo1, a)
                    transposes(ps_in, normed[:, a % 2, :], range(0, D, P), s_A1)
                if 0 <= f < TT:
                    if f == 0:
                        pe.wait_ge(s_wr, 16)
                    else:
                        pe.wait_ge(s_lg, f)
                    pe.wait_ge(s_h2T, f + 1)
                    for k in range(KD):
                        last = pe.matmul(ps_r[:, 0:E], h2T_of(f)[:, k * P:(k + 1) * P], wr_sb[:, k, :], start=k == 0,
                                         stop=k == KD - 1)
                    last.then_inc(s_F1, 1)
                if 0 <= e < TT:
                    pe.wait_ge(s_h2, e + 1)
                    if e:
                        pe.wait_ge(s_h2T, e)
                    transposes(ps_y, h2[:, e % 2, :], range(0, D, P), s_E1)
                if 0 <= d < TT:
                    pe.wait_ge(s_hlo1, d + 1)
                    if d:
                        pe.wait_ge(s_x2, d)
                    four(ps_y4, hidT_hi, hidT_lo, d % 2, s_D1)

            def rank():
                pe.wait_ge(s_taken, 1)
                pe.wait_ge(s_lg, TT)
                out = ps_r[:, 0:(TT + 1) * E].rearrange("p (t e) -> p t e", e=E)
                pe.matmul(out, below[:, :], taken[:, :, :], start=True, stop=False)
                for t in range(TT):
                    n = TT - t
                    last = pe.matmul(out[:, t + 1:, :], ones[:, :],
                                     taken[:, t, :].unsqueeze(1).to_broadcast([P, n, E]),
                                     start=False, stop=t == TT - 1)
                last.then_inc(s_rank, 1)

            def invert(out, lists):
                for c in range(C):
                    last = pe.matmul(out, place1h[:, c, :], lists[:, c, :, :], start=c == 0, stop=c == C - 1)
                return last

            def invert_tokens():
                pe.wait_ge(s_place1h_first, NPL)
                pe.wait_ge(s_place1h, 1)
                pe.wait_ge(s_tokens, 1)
                invert(inv_tok, tokens).then_inc(s_inv, 1)

            def invert_gates():
                pe.wait_ge(s_gates3, 3)
                invert(inv_gate, gates3).then_inc(s_invg, 1)

            def expert(j):
                if shared(j):
                    return 0
                return pe.value_load(te[0:1, bass.ds(j.n - TT, 1)], min_val=1, max_val=E)

            experts = {}

            def rows_in(j):
                experts[j.n] = expert(j)
                if shared(j):
                    return
                pe.wait_ge(s_gath[j.p], 16 * (j.before - TT // 2 + 1))
                if j.n > TT:
                    pe.wait_ge(s_lo, j.n)
                transposes(ps_in, rows[:, j.p, :], range(0, D, P), s_A)

            def up(j):
                pe.wait_ge(s_lo, j.n + 1)
                if j.n in (1, 2):
                    pe.wait_ge(s_hid, j.n)
                elif j.n > 2:
                    pe.wait_ge(s_hid, j.n - 1)
                e = experts[j.n]
                for half in range(2):
                    terms = [(both(inT_hi, inT_lo, j.p, k),
                              tuple(w[:, e, k * U1 + half * HP:k * U1 + (half + 1) * HP] for w in (w13_hi, w13_lo)))
                             for k in range(KD)]
                    products(up_of(j)[:, half, 0:HP], terms, s_B if half else None)

            def ffn(at, before_up=None):
                if j := at(1):
                    rows_in(j)
                if j := at(-1):
                    pe.wait_ge(s_hid, j.n + 1)
                    if not (isinstance(j.n, int) and j.n == 0):
                        pe.wait_ge(s_hlo, j.n)
                    transposes(ps_hid, hid[:, j.p, :], HC, s_C)
                if j := at(-2):
                    pe.wait_ge(s_hlo, j.n + 1)
                    if not (isinstance(j.n, int) and j.n == 0):
                        pe.wait_ge(s_y, j.n)
                    terms = [(both(hidT_hi, hidT_lo, j.p, c),
                              tuple(w[:, experts[j.n], c * D:(c + 1) * D] for w in (w2_hi, w2_lo))) for c in range(NHC)]
                    products(ps_y[:, 0:D], terms, s_D)
                if before_up is not None:
                    before_up()
                if j := at(1):
                    up(j)

            def warm_up(n, bank):
                for _ in range(n):
                    pe.matmul(bank[:, 0:P], ones[:, :], ones[:, :], start=True, stop=True)

            def before_up2():
                pe.wait_ge(s_x2, TT)
                warm_up(WARM_FFN, ps_up[1][:, 0, :])
                layer1(TT + 2)
                layer1(TT + 3)

            pe.wait_ge(s_ones, 1)
            warm_up(WARM[-1], ps_hid)
            pe.wait_ge(s_eye, 1)
            for i in range(-1, TT + 1):
                if i >= 0 and i in WARM:
                    if i >= 2:
                        pe.wait_ge(s_hlo1, min(i - 1, TT))
                    warm_up(WARM[i], ps_hid)
                layer1(i)
            ffn(peeled(0))
            layer1(TT + 1)
            ffn(peeled(1), before_up=before_up2)
            rank()
            for i in range(2, TT + 2):
                if i == TT - 1:
                    pe.wait_ge(s_te, 1)
                    pe.wait_ge(s_ulo, (E + 1) * UNITS)
                if i == 5:
                    invert_tokens()
                ffn(peeled(i), before_up=invert_gates if i == TT else None)
            pipeline(pe, TT + 2, TT + 2, TT + 2, NT + 2, NT, ffn)


def kernel(x, itok_BxS_13_99985, ctx_2048, L0_ffn_sw1, L0_ffn_sw2, L0_ffn_sw3, L0_ffn_ew1, L0_ffn_ew2, L0_ffn_ew3,
           L0_ffn_wr):
    import concourse.bacc as bacc
    import numpy as np
    from concourse.bass_utils import run_bass_kernel_spmd

    def arr(a):
        return np.ascontiguousarray(np.asarray(a))

    x, ctx = arr(x), arr(ctx_2048)
    ids = arr(itok_BxS_13_99985)
    w1 = np.concatenate([arr(L0_ffn_sw1)[None], arr(L0_ffn_ew1)])
    w3 = np.concatenate([arr(L0_ffn_sw3)[None], arr(L0_ffn_ew3)])
    w2 = np.concatenate([arr(L0_ffn_sw2)[None], arr(L0_ffn_ew2)])
    w13 = np.zeros((E + 1, D, 2, HP), w1.dtype)
    w13[..., :H] = np.stack([w1, w3], 1).transpose(0, 3, 1, 2)
    w2p = np.zeros((E + 1, NHC * P, D), w2.dtype)
    w2p[:, :(NHC - 1) * P] = w2.transpose(0, 2, 1)[:, :(NHC - 1) * P]
    w2p[:, NHC * P - LAST:] = w2.transpose(0, 2, 1)[:, (NHC - 1) * P:]
    arrays = {
        "x": x.reshape(T, D),
        "ids": arr(ids.reshape(TT, P).T),
        "ctx": arr(ctx.transpose(2, 0, 1).reshape(D, CE * D)),
        "w13": w13.reshape(E + 1, D, U1),
        "w2": w2p,
        "wr": arr(arr(L0_ffn_wr).T),
    }
    nc = bacc.Bacc("TRN2", target_bir_lowering=False, num_devices=1)
    aps = [nc.dram_tensor("in_" + n, a.shape, mybir.dt.from_np(a.dtype), kind="ExternalInput").ap() for n, a in arrays.items()]
    out = nc.dram_tensor("out", (T + P, D), fp32, kind="ExternalOutput").ap()
    build(nc, *aps, out)
    r = run_bass_kernel_spmd(nc, [{"in_" + n: a for n, a in arrays.items()}], core_ids=[0])
    return r.results[0]["out"][:T].reshape(x.shape)
```
